# Optimizing a Trainium2 kernel written in Bass

```python
import numpy as np
import jax
import jax.numpy as jnp

def _softmax(x, axis=-1):
    return jax.nn.softmax(x, axis=axis)
def _gelu(x):
    return jax.nn.gelu(x, approximate=True)
def _silu(x):
    return jax.nn.silu(x)
def _sigmoid(x):
    return jax.nn.sigmoid(x)
def _layernorm(x, axis=-1, eps=1e-5):
    m = jnp.mean(x, axis=axis, keepdims=True)
    v = jnp.var(x, axis=axis, keepdims=True)
    return (x - m) / jnp.sqrt(v + eps)
def _scatter_add(tgt, idx, src, axis=0):
    return tgt.at[idx].add(src)
def _segment_sum(src, seg, n):
    return jax.ops.segment_sum(src, seg, n)

kernel_name = 'mk_adj_preln_d2_adj_256_02dfce'

def setup_inputs(seed: int = 0):
    np.random.seed(seed)
    _w = jnp.asarray
    def _rec_inputs():
        import jax
        import jax.numpy as jnp
        _gk = jax.random.key(seed)
        x = -0.000929 + 1 * jax.random.normal(jax.random.fold_in(_gk, 1), (8192, 256), jnp.float32)
        _a = jax.random.bernoulli(jax.random.fold_in(_gk, 2), 0.000488281, (8192, 8192))
        _a = jnp.logical_or(_a, jnp.swapaxes(_a, -1, -2))
        _a = jnp.logical_or(_a, jnp.eye(8192, dtype=bool))
        adj = _a.astype(jnp.int32)
        return x, adj
    x, adj = _rec_inputs()
    def _L0_gnn_setup():
        import jax, jax.numpy as jnp
        import numpy as np
        NEG_INF = -1000000000.0
        LEAKY_SLOPE = 0.2
        key = jax.random.key(seed)
        k1, k2, k3, k4 = jax.random.split(key, 4)
        N, F_IN, F_OUT = (4096, 256, 256)
        h = jax.random.normal(k1, (N, F_IN), dtype=jnp.float32)
        adj = jax.random.randint(k2, (N, N), 0, 2, dtype=jnp.int32)
        W = jax.random.normal(k3, (F_IN, F_OUT), dtype=jnp.float32) / np.sqrt(F_IN)
        a = jax.random.normal(k4, (2 * F_OUT,), dtype=jnp.float32) / np.sqrt(2 * F_OUT)
        return {'h': h, 'adj': adj, 'W': W, 'a': a}
    _L0_gnn_all = _L0_gnn_setup()
    _L0_gnn_in = {k: v for k, v in _L0_gnn_all.items() if k in ('W', 'a', )}
    del _L0_gnn_all

    def _L1_gnn_setup():
        import jax, jax.numpy as jnp
        import numpy as np
        N, D = (8192, 256)
        NEG_BIG = -9000000000000000.0
        key = jax.random.key(seed)
        k1, k2, k3 = jax.random.split(key, 3)
        h = jax.random.normal(k1, (N, D), dtype=jnp.float32)
        adj = jax.random.randint(k2, (N, N), 0, 2, dtype=jnp.int32)
        bound = np.sqrt(6.0 / (2 * D + 1)).astype(np.float32)
        a = jax.random.uniform(k3, (2 * D, 1), dtype=jnp.float32, minval=-bound, maxval=bound)
        return {'h': h, 'adj': adj, 'a': a}
    _L1_gnn_all = _L1_gnn_setup()
    _L1_gnn_in = {k: v for k, v in _L1_gnn_all.items() if k in ('a', )}
    del _L1_gnn_all

    return {
        "x": x,
        "adj": adj,
        "L0_gnn_W": _L0_gnn_in["W"],
        "L0_gnn_a": _L0_gnn_in["a"],
        "L1_gnn_a": _L1_gnn_in["a"],
    }

def reference(x, adj, L0_gnn_W, L0_gnn_a, L1_gnn_a):
    import jax
    import jax.numpy as jnp
    def _L0_gnn_ref(h, adj, W, a):
        import jax, jax.numpy as jnp
        import numpy as np
        NEG_INF = -1000000000.0
        LEAKY_SLOPE = 0.2
        Wh = h @ W
        F_OUT = Wh.shape[1]
        e_left = Wh @ a[:F_OUT]
        e_right = Wh @ a[F_OUT:]
        e = e_left[:, None] + e_right[None, :]
        e = jnp.where(adj == 0, jnp.float32(NEG_INF), e)
        attention = jax.nn.softmax(e, axis=1)
        h_prime = attention @ Wh
        return jax.nn.leaky_relu(h_prime, negative_slope=LEAKY_SLOPE)

    def _L1_gnn_ref(h, adj, a):
        import jax, jax.numpy as jnp
        import numpy as np
        N, D = (8192, 256)
        NEG_BIG = -9000000000000000.0
        d = h.shape[1]
        h1 = h @ a[:d]
        h2 = h @ a[d:]
        e = jax.nn.leaky_relu(h1 + h2.T, negative_slope=0.01)
        attention = jnp.where(adj > 0, e, NEG_BIG)
        attention = jax.nn.softmax(attention, axis=1)
        return attention @ h

    h = jnp.maximum(_layernorm(x, axis=-1), 0.0)
    x = x + _L0_gnn_ref(h, adj, L0_gnn_W, L0_gnn_a)
    h = jnp.maximum(_layernorm(x, axis=-1), 0.0)
    x = x + _L1_gnn_ref(h, adj, L1_gnn_a)
    return x


_drawn_inputs = setup_inputs


def setup_inputs(seed=0):
    import zlib

    import numpy as np

    out = dict(_drawn_inputs(seed))
    spreads = {}
    factors = {}
    for name, (base, spread) in spreads.items():
        noise = np.random.default_rng([zlib.crc32(name.encode()), seed]).standard_normal(out[name].shape)
        drawn = base * np.exp(spread * noise) if base else spread * noise
        out[name] = jnp.asarray(drawn.astype(out[name].dtype))
    for name, factor in factors.items():
        out[name] = (out[name] * factor).astype(out[name].dtype)
    return out
```

```python
import concourse.bass as bass
from concourse import mybir
from contextlib import ExitStack


def two_layer_graph_attention(nc, x, adj, w0, a0, a1, pack_w, ident, out):
    f32, f16 = mybir.dt.float32, mybir.dt.float16
    u16, i32 = mybir.dt.uint16, mybir.dt.int32
    ALU = mybir.AluOpType
    ACT = mybir.ActivationFunctionType
    AX = mybir.AxisListType
    RMAX = bass.bass_isa.ReduceOp.max

    P = 128
    N, D = x.shape
    T = N // P
    EPS = 1e-5
    SLOPE0 = 0.2
    SLOPE1 = 0.01
    VS = 2048.0
    BITS = 16
    WPB = P // BITS
    ROW = D + 2
    DV = D + 1
    Q = 4
    QC = N // Q
    QB = QC // P
    XC = 8
    XB = 4
    LAG = 6
    NPK = 8
    NX = 4

    pk_d = nc.dram_tensor("packed_adj", (T, P, T * WPB), u16).ap()
    x1_d = nc.dram_tensor("x_after_layer0", (T, P, D), f32).ap()
    h_d = nc.dram_tensor("h_of_layer1", (T, P, ROW), f32).ap()
    h1_d = nc.dram_tensor("h1_row", (T, P), f32).ap()

    x_v = x.rearrange("(t p) d -> p t d", p=P)
    adj_v = adj.rearrange("(t p) n -> t p n", p=P)
    out_v = out.rearrange("(t p) d -> p t d", p=P)

    outer = ExitStack()
    with outer:
        def psum(name):
            return outer.enter_context(nc.psum_tensor(name, [P, 512], f32))

        bank = [psum(f"bank{i}") for i in range(8)]
        h1all = outer.enter_context(nc.sbuf_tensor("h1all", [P, T], f32))
        h2all = outer.enter_context(nc.sbuf_tensor("h2all", [P, T], f32))
        idf = outer.enter_context(nc.sbuf_tensor("idf", [P, P], f32))

        ctx = ExitStack()
        with ctx:
            def sb(name, shape, dt):
                return ctx.enter_context(nc.sbuf_tensor(name, shape, dt))

            def sem(name):
                return ctx.enter_context(nc.semaphore(name))

            H = sb("H", [P, T, ROW], f32)
            V0 = H[:, :, :].bitcast(f16).rearrange("p t (s c) -> p t s c", s=2)
            adj_i = sb("adj_i", [P, Q, QC], i32)
            adj_f = sb("adj_f", [P, 2, N], f16)
            adjT = sb("adjT", [P, 2, T, P], u16)
            adjT_h = adjT[:, :, :, :].bitcast(f16)
            pk = sb("pk", [P, NPK, T * WPB], u16)
            packw = sb("packw", [P, WPB], f16)
            w_sb = sb("w_sb", [P, 2, D], f32)
            arow = sb("arow", [P, D], f32)
            a1row = sb("a1row", [P, 2, D], f32)
            ucol = sb("ucol", [P, 2], f32)
            ulhs = sb("ulhs", [P, 2, P], f32)
            ubc = sb("ubc", [P, D], f32)
            st = sb("st", [P, XC, 6], f32)
            mv = sb("mv", [P, T, 2], f32)
            std = sb("std", [P, T], f32)
            rstd = sb("rstd", [P, T], f32)
            nmr = sb("nmr", [P, T], f32)
            r0 = sb("r0", [P, T], f32)
            rmax = sb("rmax", [P, 1], f32)
            Mb = sb("Mb", [P, 1], f32)
            nM = sb("nM", [P, 1], f32)
            p0 = sb("p0", [P, T], f32)
            p0s = sb("p0s", [P, T], f32)
            vtmp = sb("vtmp", [P, 4, ROW], f32)
            junk = sb("junk", [P, D], f32)
            eps = sb("eps", [P, 1], f32)
            xt = sb("xt", [P, NX, D], f32)
            x1 = sb("x1", [P, NX, D], f32)
            hh = sb("hh", [P, NX, ROW], f32)
            rden = sb("rden", [P, 1], f32)
            agg = sb("agg", [P, D], f32)
            aggT = sb("aggT", [P, 2, P], f32)
            ysb = sb("ysb", [P, D], f32)
            lr = sb("lr", [P, D], f32)
            st1 = sb("st1", [P, 6], f32)
            mv1 = sb("mv1", [P, 2], f32)
            h12 = sb("h12", [P, 2], f32)
            std1 = sb("std1", [P, 1], f32)
            rstd1 = sb("rstd1", [P, 1], f32)
            nmr1 = sb("nmr1", [P, 1], f32)

            pkps = [bank[0], bank[1]]
            acc = [bank[2], bank[3]]
            tps, yps = bank[4], bank[5]
            ups = bank[6]

            const_in = sem("const_in")
            x_in = [sem(f"x_in{i}") for i in range(XB)]
            adj_in = [sem(f"adj_in{i}") for i in range(Q)]
            xt_in = [sem(f"xt_in{i}") for i in range(NX)]
            ones_set = sem("ones_set")
            ucol_ready = sem("ucol_ready")
            ulhs_ready = sem("ulhs_ready")
            ups_ready = sem("ups_ready")
            ubc_ready = sem("ubc_ready")
            st_ready = sem("st_ready")
            mv_ready = sem("mv_ready")
            std_ready = sem("std_ready")
            rstd_ready = sem("rstd_ready")
            nmr_ready = sem("nmr_ready")
            h_ready = sem("h_ready")
            r_ready = sem("r_ready")
            rmax_ready = sem("rmax_ready")
            M_ready = sem("M_ready")
            nM_ready = sem("nM_ready")
            p0_ready = sem("p0_ready")
            p0s_ready = sem("p0s_ready")
            vtmp_ready = sem("vtmp_ready")
            vhi_ready = sem("vhi_ready")
            v0_ready = sem("v0_ready")
            conv_done = sem("conv_done")
            pack_done = sem("pack_done")
            pk_ready = sem("pk_ready")
            pk_out = [sem(f"pk_out{i}") for i in range(NPK)]
            adjT_ready = sem("adjT_ready")
            acc_ready = sem("acc_ready")
            rden_ready = sem("rden_ready")
            agg_ready = sem("agg_ready")
            tr_ready = sem("tr_ready")
            aggT_ready = sem("aggT_ready")
            y_ready = sem("y_ready")
            ysb_ready = sem("ysb_ready")
            lr_ready = sem("lr_ready")
            x1_ready = sem("x1_ready")
            st1_ready = sem("st1_ready")
            mv1_ready = sem("mv1_ready")
            std1_ready = sem("std1_ready")
            rstd1_ready = sem("rstd1_ready")
            nmr1_ready = sem("nmr1_ready")
            hh_ready = sem("hh_ready")
            h12_ready = sem("h12_ready")
            h12_kept = sem("h12_kept")
            x1_out = [sem(f"x1_out{i}") for i in range(NX)]
            hh_out = [sem(f"hh_out{i}") for i in range(NX)]

            block = ctx.enter_context(nc.Block())

            @block.sync
            def _(sp):
                sp.dma_start(w_sb[:, :, :], w0.rearrange("(c p) n -> p c n", p=P)).then_inc(const_in, 16)
                sp.dma_start(arow[:, :], a0[D:2 * D].rearrange("(o n) -> o n", o=1)
                             .partition_broadcast(P)).then_inc(const_in, 16)
                sp.dma_start(a1row[:, :, :], a1.rearrange("(o s n) b -> o s (n b)", o=1, s=2)
                             .partition_broadcast(P)).then_inc(const_in, 16)
                sp.dma_start(packw[:, :], pack_w).then_inc(const_in, 16)
                sp.dma_start(idf[:, :], ident).then_inc(const_in, 16)
                for c in range(T // XC):
                    if c >= XB:
                        sp.wait_ge(x_in[c % XB], c // XB * 16)
                    sp.dma_start(H[:, c * XC:(c + 1) * XC, 0:D],
                                 x_v[:, c * XC:(c + 1) * XC, :]).then_inc(x_in[c % XB], 16)

                def load(t, b, first):
                    for q in range(Q):
                        if not first:
                            sp.wait_ge(conv_done, t * Q - Q + q + 1)
                        sp.dma_start(adj_i[:, q, :], adj_v[bass.ds(t, 1), :, q * QC:(q + 1) * QC]
                                     .rearrange("o p n -> p (o n)")).then_inc(adj_in[q], 16)

                def load_x(t, b, first):
                    if not first:
                        sp.wait_ge(x1_ready, t - NX + 1)
                    sp.dma_start(xt[:, b, :], x_v[:, bass.ds(t, 1), :]
                                 .rearrange("p o d -> p (o d)")).then_inc(xt_in[b], 16)

                def store(t, b, pb):
                    sp.wait_ge(pk_ready, t + 1)
                    sp.dma_start(pk_d[bass.ds(t, 1), :, :].rearrange("o p n -> p (o n)"),
                                 pk[:, pb, :]).then_inc(pk_out[pb], 16)
                    sp.wait_ge(x1_ready, t + 1)
                    sp.dma_start(x1_d[bass.ds(t, 1), :, :].rearrange("o p n -> p (o n)"),
                                 x1[:, b, :]).then_inc(x1_out[b], 16)
                    sp.wait_ge(hh_ready, t + 1)
                    sp.dma_start(h_d[bass.ds(t, 1), :, :].rearrange("o p n -> p (o n)"),
                                 hh[:, b, :]).then_inc(hh_out[b], 16)

                for t in range(NPK):
                    load(t, t % NX, t == 0)
                    load_x(t, t % NX, t < NX)
                    if t >= LAG:
                        store(t - LAG, (t - LAG) % NX, (t - LAG) % NPK)
                with sp.Fori(1, T // NPK) as k:
                    for j in range(NPK):
                        t = k * NPK + j
                        load(t, j % NX, False)
                        load_x(t, j % NX, False)
                        store(t - LAG, (j - LAG) % NX, (j - LAG) % NPK)
                for t in range(T - LAG, T):
                    store(t, t % NX, t % NPK)
                for b in range(NPK):
                    sp.wait_ge(pk_out[b], 16 * (T // NPK))
                for b in range(NX):
                    sp.wait_ge(x1_out[b], 16 * (T // NX))
                    sp.wait_ge(hh_out[b], 16 * (T // NX))

            @block.gpsimd
            def _(pool):
                nc.gpsimd.memset(hh[:, :, D:ROW], 1.0).then_inc(ones_set, 1)
                nc.gpsimd.memset(H[:, :, D:ROW], 1.0).then_inc(ones_set, 1)
                nc.gpsimd.memset(eps[:, :], EPS).then_inc(ones_set, 1)
                pool.wait_ge(rmax_ready, 1)
                nc.gpsimd.partition_all_reduce(Mb[:, :], rmax[:, :], P, RMAX).then_inc(M_ready, 1)

            @block.scalar
            def _(act):
                act.wait_ge(ones_set, 3)
                for c in range(T // XC):
                    act.wait_ge(mv_ready, XC * (c + 1))
                    nc.scalar.activation(std[:, c * XC:(c + 1) * XC], mv[:, c * XC:(c + 1) * XC, 1],
                                         ACT.Sqrt, bias=eps[:, :]).then_inc(std_ready, 1)
                    act.wait_ge(nmr_ready, c + 1)
                    with act.Fori(c * XC, c * XC + XC) as t:
                        nc.scalar.activation(H[:, t, 0:D], H[:, t, 0:D], ACT.Relu,
                                             scale=rstd[:, bass.ds(t, 1)],
                                             bias=nmr[:, bass.ds(t, 1)]).then_inc(h_ready, 1)

                def convert(t, b, qs, first):
                    for q in qs:
                        act.wait_ge(adj_in[q], (t + 1) * 16)
                        if not first and q == qs[0]:
                            act.wait_ge(pack_done, t - 1)
                        nc.scalar.activation(adj_f[:, b, q * QC:(q + 1) * QC], adj_i[:, q, :],
                                             ACT.Copy).then_inc(conv_done, 1)

                convert(0, 0, range(Q), True)
                act.wait_ge(nM_ready, 1)
                nc.scalar.activation(p0[:, :], r0[:, :], ACT.Exp, bias=nM[:, :]).then_inc(p0_ready, 1)
                act.wait_ge(p0s_ready, 1)
                def weigh(t, j, first):
                    if not first:
                        act.wait_ge(v0_ready, t - 3)
                    nc.scalar.activation(vtmp[:, j, :], H[:, t, :], ACT.Copy,
                                         scale=p0s[:, bass.ds(t, 1)]).then_inc(vtmp_ready, 1)

                for t in range(4):
                    weigh(t, t, True)
                with act.Fori(1, T // 4) as k:
                    for j in range(4):
                        weigh(k * 4 + j, j, False)
                convert(1, 1, range(Q), True)

                def finish(t, b):
                    act.wait_ge(y_ready, t + 1)
                    nc.scalar.activation(ysb[:, :], yps[:, 0:D], ACT.Copy).then_inc(ysb_ready, 1)
                    act.wait_ge(mv1_ready, t + 1)
                    nc.scalar.activation(std1[:, :], mv1[:, 1:2], ACT.Sqrt, bias=eps[:, :])\
                        .then_inc(std1_ready, 1)
                    act.wait_ge(nmr1_ready, t + 1)
                    nc.scalar.activation(hh[:, b, 0:D], x1[:, b, :], ACT.Relu, scale=rstd1[:, :],
                                         bias=nmr1[:, :]).then_inc(hh_ready, 1)

                def copy_aggT(t):
                    act.wait_ge(tr_ready, t + 1)
                    nc.scalar.activation(aggT[:, :, :].rearrange("p c n -> p (c n)"), tps[:, 0:D],
                                         ACT.Copy).then_inc(aggT_ready, 1)

                def step(t, j, reuse, t_has_tail=True):
                    convert(t + 2, j % 2, range(0, Q // 2), False)
                    if t_has_tail:
                        copy_aggT(t - 1)
                    convert(t + 2, j % 2, range(Q // 2, Q), False)
                    if t_has_tail:
                        if reuse is not None:
                            act.wait_ge(hh_out[(j - 1) % NX], reuse)
                        finish(t - 1, (j - 1) % NX)

                step(0, 0, None, t_has_tail=False)
                for t in range(1, NX + 1):
                    step(t, t % NX, None)
                for t in range(NX + 1, 2 * NX):
                    step(t, t % NX, 16)
                with act.Fori(2, T // NX - 1) as k:
                    for j in range(NX):
                        step(k * NX + j, j, k * 16 - 16 if j == 0 else k * 16)
                last = T // NX - 1
                for j in range(NX):
                    t = last * NX + j
                    if t + 2 < T:
                        step(t, j, 16 * (last - 1) if j == 0 else 16 * last)
                    else:
                        copy_aggT(t - 1)
                        act.wait_ge(hh_out[(j - 1) % NX], 16 * last)
                        finish(t - 1, (j - 1) % NX)
                copy_aggT(T - 1)
                act.wait_ge(hh_out[NX - 1], 16 * last)
                finish(T - 1, NX - 1)

            @block.vector
            def _(dve):
                dve.wait_ge(const_in, 16 * 5)
                for c in range(2):
                    nc.vector.tensor_tensor_reduce(out=junk[:, :], in0=w_sb[:, c, :], in1=arow[:, :],
                                                   scale=1.0, scalar=0.0, op0=ALU.mult, op1=ALU.add,
                                                   accum_out=ucol[:, c:c + 1]).then_inc(ucol_ready, 1)
                    dve.wait_ge(ucol_ready, c + 1)
                for c in range(2):
                    nc.vector.tensor_copy(ulhs[:, c, :], ucol[:, c:c + 1].to_broadcast([P, P]))\
                        .then_inc(ulhs_ready, 1)
                dve.wait_ge(ups_ready, 1)
                nc.vector.tensor_copy(ubc[:, :], ups[:, 0:D]).then_inc(ubc_ready, 1)
                dve.wait_ge(ubc_ready, 1)

                def dots(c):
                    for t in range(c * XC, c * XC + XC):
                        dve.wait_ge(h_ready, t + 1)
                        if t:
                            dve.wait_ge(r_ready, t)
                        nc.vector.tensor_tensor_reduce(out=junk[:, :], in0=H[:, t, 0:D], in1=ubc[:, :],
                                                       scale=1.0, scalar=0.0, op0=ALU.mult,
                                                       op1=ALU.add, accum_out=r0[:, t:t + 1])\
                            .then_inc(r_ready, 1)

                for c in range(T // XC):
                    cs = slice(c * XC, (c + 1) * XC)
                    dve.wait_ge(x_in[c % XB], 16 * (c // XB + 1))
                    for j in range(XC):
                        if c and j == 0:
                            dve.wait_ge(mv_ready, c * XC)
                        nc.vector.bn_stats(st[:, j, :], H[:, c * XC + j, 0:D]).then_inc(st_ready, 1)
                    for j in range(XC):
                        dve.wait_ge(st_ready, c * XC + j + 1)
                        nc.vector.bn_aggr(mv[:, c * XC + j, :], st[:, j, :]).then_inc(mv_ready, 1)
                    dve.wait_ge(std_ready, c + 1)
                    nc.vector.reciprocal(rstd[:, cs], std[:, cs]).then_inc(rstd_ready, 1)
                    dve.wait_ge(mv_ready, (c + 1) * XC)
                    dve.wait_ge(rstd_ready, c + 1)
                    nc.vector.scalar_tensor_tensor(nmr[:, cs], mv[:, cs, 0], -1.0, rstd[:, cs],
                                                   ALU.mult, ALU.mult).then_inc(nmr_ready, 1)
                    if c:
                        dots(c - 1)
                dots(T // XC - 1)
                dve.wait_ge(r_ready, T)
                nc.vector.reduce_max(rmax[:, :], r0[:, :], AX.X).then_inc(rmax_ready, 1)

                def take_packed(t, b, pb, reuse):
                    dve.wait_ge(pack_done, t + 1)
                    if reuse is not None:
                        dve.wait_ge(pk_out[pb], reuse)
                    nc.vector.tensor_copy(pk[:, pb, :], pkps[b][:, :]).then_inc(pk_ready, 1)
                    dve.wait_ge(pk_ready, t + 1)
                    words = pk[:, pb, :].rearrange("p (t w) -> p t w", w=WPB)
                    for k in range(BITS):
                        dst = adjT[:, b, :, k * WPB:(k + 1) * WPB]
                        if k <= 14:
                            i = nc.vector.tensor_scalar(dst, words, 1 << k, 14 - k, ALU.bitwise_and,
                                                        ALU.logical_shift_left)
                        else:
                            i = nc.vector.tensor_scalar(dst, words, 1 << k, k - 14, ALU.bitwise_and,
                                                        ALU.logical_shift_right)
                    i.then_inc(adjT_ready, 1)

                take_packed(0, 0, 0, None)
                dve.wait_ge(M_ready, 1)
                nc.vector.tensor_scalar(nM[:, :], Mb[:, :], -1.0, None, ALU.mult).then_inc(nM_ready, 1)
                dve.wait_ge(p0_ready, 1)
                nc.vector.tensor_scalar(p0s[:, :], p0[:, :], VS, None, ALU.mult).then_inc(p0s_ready, 1)
                with dve.Fori(0, T // 4) as k:
                    for j in range(4):
                        t = k * 4 + j
                        dve.wait_ge(vtmp_ready, t + 1)
                        nc.vector.tensor_copy(V0[:, t, 0, :], vtmp[:, j, :]).then_inc(vhi_ready, 1)
                        dve.wait_ge(vhi_ready, t + 1)
                        nc.vector.tensor_tensor(V0[:, t, 1, :], vtmp[:, j, :], V0[:, t, 0, :],
                                                ALU.subtract).then_inc(v0_ready, 1)

                def normalise(t, b):
                    dve.wait_ge(acc_ready, t + 1)
                    nc.vector.reciprocal(rden[:, :], acc[b][:, D:DV]).then_inc(rden_ready, 1)
                    dve.wait_ge(rden_ready, t + 1)
                    nc.vector.tensor_scalar(agg[:, :], acc[b][:, 0:D], rden[:, :], None, ALU.mult)\
                        .then_inc(agg_ready, 1)

                def keep_dots(t):
                    nc.vector.tensor_copy(h1all[:, bass.ds(t, 1)], h12[:, 0:1]).then_inc(h12_kept, 1)
                    nc.vector.tensor_copy(h2all[:, bass.ds(t, 1)], h12[:, 1:2]).then_inc(h12_kept, 1)

                def finish(t, b, n_in, reuse, kept):
                    dve.wait_ge(ysb_ready, t + 1)
                    nc.vector.scalar_tensor_tensor(lr[:, :], ysb[:, :], SLOPE0, ysb[:, :], ALU.mult,
                                                   ALU.max).then_inc(lr_ready, 1)
                    dve.wait_ge(lr_ready, t + 1)
                    dve.wait_ge(xt_in[b], n_in)
                    if reuse is not None:
                        dve.wait_ge(x1_out[b], reuse)
                    nc.vector.tensor_tensor(x1[:, b, :], lr[:, :], xt[:, b, :], ALU.add)\
                        .then_inc(x1_ready, 1)
                    dve.wait_ge(x1_ready, t + 1)
                    nc.vector.bn_stats(st1[:, :], x1[:, b, :]).then_inc(st1_ready, 1)
                    dve.wait_ge(st1_ready, t + 1)
                    if kept is not None:
                        keep_dots(t - 1)
                    nc.vector.bn_aggr(mv1[:, :], st1[:, :]).then_inc(mv1_ready, 1)
                    dve.wait_ge(std1_ready, t + 1)
                    nc.vector.reciprocal(rstd1[:, :], std1[:, :]).then_inc(rstd1_ready, 1)
                    dve.wait_ge(mv1_ready, t + 1)
                    dve.wait_ge(rstd1_ready, t + 1)
                    nc.vector.scalar_tensor_tensor(nmr1[:, :], mv1[:, 0:1], -1.0, rstd1[:, :],
                                                   ALU.mult, ALU.mult).then_inc(nmr1_ready, 1)
                    dve.wait_ge(hh_ready, t + 1)
                    if kept is not None:
                        dve.wait_ge(h12_kept, kept)
                    for s in range(2):
                        nc.vector.tensor_tensor_reduce(out=junk[:, :], in0=hh[:, b, 0:D],
                                                       in1=a1row[:, s, :], scale=1.0, scalar=0.0,
                                                       op0=ALU.mult, op1=ALU.add,
                                                       accum_out=h12[:, s:s + 1])\
                            .then_inc(h12_ready, 1)
                        dve.wait_ge(h12_ready, 2 * t + s + 1)

                def step(t, j, pk_reuse, n_in, x1_reuse, kept, ahead=True):
                    if n_in is not None:
                        normalise(t - 1, (j - 1) % 2)
                    if ahead:
                        take_packed(t + 1, (j + 1) % 2, (j + 1) % NPK, pk_reuse)
                    if n_in is not None:
                        finish(t - 1, (j - 1) % NX, n_in, x1_reuse, kept)

                def counts(t):
                    return (16 * ((t + 1) // NPK) or None, 16 * ((t - 1) // NX + 1),
                            16 * ((t - 1) // NX) or None, 2 * (t - 1) or None)

                step(0, 0, None, None, None, None)
                for t in range(1, NPK):
                    step(t, t, *counts(t))
                with dve.Fori(1, T // NPK - 1) as k:
                    for j in range(NPK):
                        done = (j - 1) // NX
                        step(k * NPK + j, j, k * 16 + 16 if j == NPK - 1 else k * 16,
                             k * 32 + 16 * (done + 1), k * 32 + 16 * done,
                             k * 2 * NPK + 2 * (j - 1))
                for j in range(NPK):
                    t = T - NPK + j
                    step(t, j, *counts(t), ahead=t + 1 < T)
                normalise(T - 1, 1)
                finish(T - 1, NX - 1, *counts(T)[1:])
                keep_dots(T - 1)

            @block.tensor
            def _(pe):
                pe.wait_ge(const_in, 16 * 5)
                pe.wait_ge(ulhs_ready, 2)
                for c in range(2):
                    last = nc.tensor.matmul(ups[:, c * P:(c + 1) * P], ulhs[:, c, :], idf[:, :],
                                            start=True, stop=True)
                last.then_inc(ups_ready, 1)

                def pack(t, b, first):
                    if not first:
                        pe.wait_ge(pk_ready, t - 1)
                    for q in range(Q):
                        pe.wait_ge(conv_done, t * Q + q + 1)
                        for jb in range(q * QB, (q + 1) * QB):
                            last = nc.tensor.matmul(pkps[b][:, jb * WPB:(jb + 1) * WPB],
                                                    adj_f[:, b, jb * P:(jb + 1) * P], packw[:, :],
                                                    start=True, stop=True)
                    last.then_inc(pack_done, 1)

                def transpose_agg(t):
                    pe.wait_ge(agg_ready, t + 1)
                    for c in range(2):
                        last = nc.tensor.transpose(tps[:, c * P:(c + 1) * P],
                                                   agg[:, c * P:(c + 1) * P], idf[:, :])
                    last.then_inc(tr_ready, 1)

                def project(t):
                    pe.wait_ge(aggT_ready, t + 1)
                    for c in range(2):
                        last = nc.tensor.matmul(yps[:, 0:D], aggT[:, c, :], w_sb[:, c, :],
                                                start=(c == 0), stop=(c == 1))
                    last.then_inc(y_ready, 1)

                def aggregate(t, b, v0_wait=False, reuse=True, tail=True):
                    pe.wait_ge(adjT_ready, t + 1)
                    if reuse:
                        pe.wait_ge(agg_ready, t - 1)
                    for jb in range(T):
                        if v0_wait:
                            pe.wait_ge(v0_ready, jb + 1)
                        for s in range(2):
                            last = nc.tensor.matmul(acc[b][:, 0:DV], adjT_h[:, b, jb, :],
                                                    V0[:, jb, s, 0:DV], start=(jb == 0 and s == 0),
                                                    stop=(jb == T - 1 and s == 1))
                        if tail and jb == T // 4:
                            transpose_agg(t - 1)
                        if tail and jb == 3 * T // 4:
                            project(t - 1)
                    last.then_inc(acc_ready, 1)

                pack(0, 0, True)
                pack(1, 1, True)
                aggregate(0, 0, v0_wait=True, reuse=False, tail=False)
                pack(2, 0, False)
                aggregate(1, 1, reuse=False)
                with pe.Fori(1, T // 2 - 1) as k:
                    for b in range(2):
                        pack(k * 2 + b + 1, (b + 1) % 2, False)
                        aggregate(k * 2 + b, b)
                pack(T - 1, 1, False)
                aggregate(T - 2, 0)
                aggregate(T - 1, 1)
                transpose_agg(T - 1)
                project(T - 1)

        G = 4
        NG = T // G
        GC = G * P
        CB = 8
        NC = T // CB
        HS = 4
        ctx = ExitStack()
        with ctx:
            def sb(name, shape, dt):
                return ctx.enter_context(nc.sbuf_tensor(name, shape, dt))

            def sem(name):
                return ctx.enter_context(nc.semaphore(name))

            Vp = sb("Vp", [P, T, 2, ROW], f16)
            Vn = sb("Vn", [P, T, 2, ROW], f16)
            adjn = sb("adjn", [P, 2, CB, GC], u16)
            adjn_h = adjn[:, :, :, :].bitcast(f16)
            adjp = sb("adjp", [P, 2, CB, GC], f16)
            pkg = sb("pkg", [P, 2, G, T * WPB], u16)
            h1bc = sb("h1bc", [P, 2, GC], f32)
            hs = sb("hs", [P, HS, ROW], f32)
            x1g = sb("x1g", [P, G, D], f32)
            evp = sb("evp", [P, G, DV], f32)
            evn = sb("evn", [P, G, DV], f32)
            h1T = sb("h1T", [T, P], f32)
            M1 = sb("M1", [P, 6], f32)
            E = sb("E", [P, 2, T], f32)
            Es = sb("Es", [P, 2, T], f32)
            nh2 = sb("nh2", [P, T], f32)
            sM = sb("sM", [P, 2, T], f32)
            tM = sb("tM", [P, T], f32)
            dM = sb("dM", [P, 2, T], f32)
            ab = sb("ab", [P, 2, T], f32)
            den2 = sb("den2", [P, 2, G], f32)
            den = sb("den", [P, G], f32)
            rd = sb("rd", [P, G], f32)
            fac = sb("fac", [P, 2, G], f32)

            h_in = [sem(f"h_in{i}") for i in range(HS)]
            pkg_in = [sem(f"pkg_in{i}") for i in range(2)]
            h1bc_in = [sem(f"h1bc_in{i}") for i in range(2)]
            x1g_in = sem("x1g_in")
            h1T_ps = sem("h1T_ps")
            h1T_sb = sem("h1T_sb")
            h1_out = sem("h1_out")
            mx_ready = sem("mx_ready")
            M_all = sem("M_all")
            negM_ready = sem("negM_ready")
            E_ready = sem("E_ready")
            Es_ready = sem("Es_ready")
            sM_ready = sem("sM_ready")
            s01_ready = sem("s01_ready")
            tM_ready = sem("tM_ready")
            dM_ready = sem("dM_ready")
            ab_ready = sem("ab_ready")
            vhi1_ready = sem("vhi1_ready")
            v_ready = sem("v_ready")
            bits_ready = sem("bits_ready")
            pos_ready = sem("pos_ready")
            neg_ready = sem("neg_ready")
            chunk_used = sem("chunk_used")
            evp_ready = sem("evp_ready")
            evn_ready = sem("evn_ready")
            den2_ready = sem("den2_ready")
            den_ready = sem("den_ready")
            rd_ready = sem("rd_ready")
            fac_ready = sem("fac_ready")
            on_ready = sem("on_ready")
            op_ready = sem("op_ready")
            o_ready = sem("o_ready")
            o_out = sem("o_out")

            block = ctx.enter_context(nc.Block())

            @block.sync
            def _(sp):
                def load_words(g, b):
                    sp.dma_start(pkg[:, b, :, :], pk_d[bass.ds(g * G, G), :, :]
                                 .rearrange("g p n -> p g n")).then_inc(pkg_in[b], 16)

                def load_h1(g, b):
                    sp.dma_start(h1bc[:, b, :], h1_d[bass.ds(g * G, G), :]
                                 .rearrange("g p -> (g p)").rearrange("(o n) -> o n", o=1)
                                 .partition_broadcast(P)).then_inc(h1bc_in[b], 16)

                for b in range(HS):
                    sp.dma_start(hs[:, b, :], h_d[b]).then_inc(h_in[b], 16)
                load_words(0, 0)
                load_words(1, 1)
                sp.wait_ge(h1T_sb, 1)
                sp.dma_start(h1_d, h1T[:, :]).then_inc(h1_out, 16)
                sp.wait_ge(h1_out, 16)
                load_h1(0, 0)
                load_h1(1, 1)
                with sp.Fori(1, T // HS) as k:
                    for b in range(HS):
                        sp.wait_ge(v_ready, (k - 1) * (2 * HS) + 2 * b + 2)
                        sp.dma_start(hs[:, b, :], h_d[bass.ds(k * HS + b, 1), :, :]
                                     .rearrange("o p n -> p (o n)")).then_inc(h_in[b], 16)

                def group(g, b, ahead, first):
                    if not first:
                        sp.wait_ge(o_out, g * 16)
                    sp.dma_start(x1g[:, :, :], x1_d[bass.ds(g * G, G), :, :]
                                 .rearrange("g p n -> p g n")).then_inc(x1g_in, 16)
                    if ahead:
                        sp.wait_ge(pos_ready, g * NC + NC)
                        load_words(g + 2, b)
                        load_h1(g + 2, b)
                    sp.wait_ge(o_ready, g * G + G)
                    sp.dma_start(out_v[:, bass.ds(g * G, G), :], x1g[:, :, :]).then_inc(o_out, 16)

                group(0, 0, True, True)
                group(1, 1, True, False)
                with sp.Fori(1, NG // 2 - 1) as k:
                    for b in range(2):
                        group(k * 2 + b, b, True, False)
                group(NG - 2, 0, False, False)
                group(NG - 1, 1, False, False)
                sp.wait_ge(o_out, NG * 16)

            @block.gpsimd
            def _(pool):
                pool.wait_ge(mx_ready, 1)
                nc.gpsimd.partition_all_reduce(M1[:, 1:2], M1[:, 0:1], P, RMAX).then_inc(M_all, 1)

            @block.scalar
            def _(act):
                act.wait_ge(negM_ready, 2)
                nc.scalar.activation(E[:, 0, :], h2all[:, :], ACT.Exp, bias=M1[:, 2:3])\
                    .then_inc(E_ready, 1)
                nc.scalar.activation(E[:, 1, :], h2all[:, :], ACT.Exp, scale=SLOPE1, bias=M1[:, 3:4])\
                    .then_inc(E_ready, 1)
                act.wait_ge(dM_ready, 2)
                nc.scalar.activation(ab[:, :, :], dM[:, :, :], ACT.Exp).then_inc(ab_ready, 1)
                act.wait_ge(Es_ready, 1)
                with act.Fori(0, T // HS) as k:
                    for j in range(HS):
                        t = k * HS + j
                        act.wait_ge(h_in[j], k * 16 + 16)
                        nc.scalar.activation(Vp[:, t, 0, :], hs[:, j, :], ACT.Copy,
                                             scale=Es[:, 0, bass.ds(t, 1)]).then_inc(vhi1_ready, 1)
                        nc.scalar.activation(Vn[:, t, 0, :], hs[:, j, :], ACT.Copy,
                                             scale=Es[:, 1, bass.ds(t, 1)]).then_inc(vhi1_ready, 1)

                def group(g, first):
                    act.wait_ge(chunk_used, g * NC + NC)
                    if not first:
                        act.wait_ge(op_ready, g * G)
                    for i in range(G):
                        nc.scalar.activation(evn[:, i, :], bank[2 * i + 1][:, 0:DV], ACT.Copy)\
                            .then_inc(evn_ready, 1)
                    act.wait_ge(fac_ready, g * 2 + 2)
                    act.wait_ge(evn_ready, g * G + G)
                    for i in range(G):
                        nc.scalar.activation(evn[:, i, 0:D], evn[:, i, 0:D], ACT.Copy,
                                             scale=fac[:, 1, i:i + 1]).then_inc(on_ready, 1)

                group(0, True)
                with act.Fori(1, NG) as g:
                    group(g, False)

            @block.vector
            def _(dve):
                nc.vector.reduce_max(M1[:, 0:1], h2all[:, :], AX.X).then_inc(mx_ready, 1)
                dve.wait_ge(h1T_ps, 1)
                nc.vector.tensor_copy(h1T[:, :], bank[7][0:T, 0:P]).then_inc(h1T_sb, 1)
                nc.vector.tensor_scalar(nh2[:, :], h2all[:, :], -1.0, None, ALU.mult)
                dve.wait_ge(M_all, 1)
                nc.vector.tensor_scalar(M1[:, 2:3], M1[:, 1:2], -1.0, None, ALU.mult)\
                    .then_inc(negM_ready, 1)
                nc.vector.tensor_scalar(M1[:, 3:4], M1[:, 1:2], -SLOPE1, None, ALU.mult)\
                    .then_inc(negM_ready, 1)
                nc.vector.tensor_scalar(sM[:, 0, :], h1all[:, :], M1[:, 1:2], None, ALU.add)\
                    .then_inc(sM_ready, 1)
                dve.wait_ge(sM_ready, 1)
                nc.vector.tensor_scalar(sM[:, 1, :], sM[:, 0, :], SLOPE1, None, ALU.mult)\
                    .then_inc(s01_ready, 1)
                dve.wait_ge(s01_ready, 1)
                nc.vector.tensor_tensor(tM[:, :], sM[:, 0, :], sM[:, 1, :], ALU.max).then_inc(tM_ready, 1)
                dve.wait_ge(tM_ready, 1)
                for s in range(2):
                    nc.vector.tensor_tensor(dM[:, s, :], sM[:, s, :], tM[:, :], ALU.subtract)\
                        .then_inc(dM_ready, 1)
                dve.wait_ge(E_ready, 2)
                nc.vector.tensor_scalar(Es[:, :, :], E[:, :, :], VS, None, ALU.mult).then_inc(Es_ready, 1)
                dve.wait_ge(Es_ready, 1)

                def low_halves(t, j):
                    for s, V in ((0, Vp), (1, Vn)):
                        dve.wait_ge(vhi1_ready, 2 * t + s + 1)
                        nc.vector.scalar_tensor_tensor(V[:, t, 1, :], hs[:, j, :],
                                                       Es[:, s, bass.ds(t, 1)], V[:, t, 0, :],
                                                       ALU.mult, ALU.subtract).then_inc(v_ready, 1)

                def split_chunk(n, b, g2, c, reuse):
                    if reuse:
                        dve.wait_ge(chunk_used, n - 1)
                    words = pkg[:, g2, :, :].rearrange("p g (t w) -> p t g w", w=WPB)
                    for k in range(BITS):
                        dst = adjn[:, b, :, :].rearrange("p t (g i) -> p t g i", g=G)\
                            [:, :, :, k * WPB:(k + 1) * WPB]
                        src = words[:, c * CB:(c + 1) * CB, :, :]
                        if k <= 14:
                            i = nc.vector.tensor_scalar(dst, src, 1 << k, 14 - k, ALU.bitwise_and,
                                                        ALU.logical_shift_left)
                        else:
                            i = nc.vector.tensor_scalar(dst, src, 1 << k, k - 14, ALU.bitwise_and,
                                                        ALU.logical_shift_right)
                    i.then_inc(bits_ready, 1)
                    dve.wait_ge(bits_ready, n + 1)
                    for jb in range(CB):
                        j = c * CB + jb
                        i = nc.vector.scalar_tensor_tensor(adjp[:, b, jb, :], h1bc[:, g2, :],
                                                           nh2[:, j:j + 1], adjn_h[:, b, jb, :],
                                                           ALU.is_ge, ALU.mult)
                    i.then_inc(pos_ready, 1)
                    dve.wait_ge(pos_ready, n + 1)
                    nc.vector.tensor_tensor(adjn_h[:, b, :, :].rearrange("p t i -> p (t i)"),
                                            adjn_h[:, b, :, :].rearrange("p t i -> p (t i)"),
                                            adjp[:, b, :, :].rearrange("p t i -> p (t i)"),
                                            ALU.subtract).then_inc(neg_ready, 1)

                def finish(g, first):
                    dve.wait_ge(chunk_used, g * NC + NC)
                    for i in range(G):
                        nc.vector.tensor_copy(evp[:, i, :], bank[2 * i][:, 0:DV]).then_inc(evp_ready, 1)
                    dve.wait_ge(evp_ready, g * G + G)
                    dve.wait_ge(evn_ready, g * G + G)
                    for s, ev in ((0, evp), (1, evn)):
                        nc.vector.tensor_tensor(den2[:, s, :], ab[:, s, bass.ds(g * G, G)],
                                                ev[:, :, D], ALU.mult).then_inc(den2_ready, 1)
                    dve.wait_ge(den2_ready, g * 2 + 2)
                    nc.vector.tensor_tensor(den[:, :], den2[:, 0, :], den2[:, 1, :], ALU.add)\
                        .then_inc(den_ready, 1)
                    dve.wait_ge(den_ready, g + 1)
                    nc.vector.reciprocal(rd[:, :], den[:, :]).then_inc(rd_ready, 1)
                    dve.wait_ge(rd_ready, g + 1)
                    for s in range(2):
                        nc.vector.tensor_tensor(fac[:, s, :], ab[:, s, bass.ds(g * G, G)], rd[:, :],
                                                ALU.mult).then_inc(fac_ready, 1)
                    dve.wait_ge(fac_ready, g * 2 + 2)
                    for i in range(G):
                        dve.wait_ge(on_ready, g * G + i + 1)
                        nc.vector.scalar_tensor_tensor(evp[:, i, 0:D], evp[:, i, 0:D],
                                                       fac[:, 0, i:i + 1], evn[:, i, 0:D],
                                                       ALU.mult, ALU.add).then_inc(op_ready, 1)
                    dve.wait_ge(x1g_in, g * 16 + 16)
                    for i in range(G):
                        dve.wait_ge(op_ready, g * G + i + 1)
                        nc.vector.tensor_tensor(x1g[:, i, :], x1g[:, i, :], evp[:, i, 0:D], ALU.add)\
                            .then_inc(o_ready, 1)

                dve.wait_ge(ab_ready, 1)
                dve.wait_ge(pkg_in[0], 16)
                dve.wait_ge(h1bc_in[0], 16)
                for c in range(NC):
                    split_chunk(c, c % 2, 0, c, c >= 2)
                    for j in range(CB):
                        low_halves(c * CB + j, j % HS)

                def group(g, g2, n_in):
                    dve.wait_ge(pkg_in[g2], n_in)
                    dve.wait_ge(h1bc_in[g2], n_in)
                    for c in range(NC):
                        split_chunk(g * NC + c, c % 2, g2, c, True)
                        if c == 0:
                            finish(g - 1, False)

                group(1, 1, 16)
                with dve.Fori(1, NG // 2) as k:
                    for g2 in range(2):
                        group(k * 2 + g2, g2, k * 16 + 16)
                finish(NG - 1, False)

            @block.tensor
            def _(pe):
                nc.tensor.transpose(bank[7][0:T, 0:P], h1all[:, :], idf[:, :]).then_inc(h1T_ps, 1)

                def group(g, first):
                    for c in range(NC):
                        n = g * NC + c
                        b = c % 2
                        pe.wait_ge(neg_ready, n + 1)
                        for jb in range(CB):
                            j = c * CB + jb
                            if first:
                                pe.wait_ge(v_ready, 2 * j + 2)
                            for i in range(G):
                                for part, (m, V) in enumerate(((adjp, Vp), (adjn_h, Vn))):
                                    if j == 0:
                                        if first and i == 0 and part == 0:
                                            pe.wait_ge(h1T_sb, 1)
                                        if not first:
                                            pe.wait_ge(evn_ready if part else evp_ready,
                                                       g * G - G + i + 1)
                                    for s in range(2):
                                        last = nc.tensor.matmul(
                                            bank[2 * i + part][:, 0:DV],
                                            m[:, b, jb, i * P:(i + 1) * P], V[:, j, s, 0:DV],
                                            start=(j == 0 and s == 0), stop=(j == T - 1 and s == 1))
                        last.then_inc(chunk_used, 1)

                group(0, True)
                with pe.Fori(1, NG) as g:
                    group(g, False)


_INS = ['x', 'adj', 'L0_gnn_W', 'L0_gnn_a', 'L1_gnn_a']


def kernel(**inputs):
    import numpy as np
    import concourse.bacc as bacc
    from concourse import mybir as _mybir
    from concourse.bass_utils import run_bass_kernel_spmd as run

    nc = bacc.Bacc("TRN2", target_bir_lowering=False, num_devices=1)
    arrays, args = {}, []

    def add(name, a):
        arrays[name] = a
        args.append(nc.dram_tensor(name, a.shape, _mybir.dt.from_np(a.dtype), kind="ExternalInput").ap())

    for name in _INS:
        add(f"in_{name}", np.ascontiguousarray(inputs[name]))
    rows = np.arange(128)
    pack_w = np.zeros((128, 8), np.float16)
    pack_w[rows, rows % 8] = 2.0 ** (rows // 8)
    add("pack_w", pack_w)
    add("ident", np.eye(128, dtype=np.float32))
    out = nc.dram_tensor("out", inputs["x"].shape, _mybir.dt.float32, kind="ExternalOutput").ap()
    two_layer_graph_attention(nc, *args, out)
    r = run(nc, [arrays], core_ids=[0])
    return r.results[0]["out"]
```

```python
import concourse.bass as bass
from concourse import mybir
from contextlib import ExitStack


def two_layer_graph_attention(nc, x, adj, w0, a0, a1, pack_w, key_w, key_pos, ident, out):
    f32, f16 = mybir.dt.float32, mybir.dt.float16
    bf16, u16, i32 = mybir.dt.bfloat16, mybir.dt.uint16, mybir.dt.int32
    ALU = mybir.AluOpType
    ACT = mybir.ActivationFunctionType
    AX = mybir.AxisListType
    RMAX = bass.bass_isa.ReduceOp.max

    P = 128
    N, D = x.shape
    T = N // P
    EPS = 1e-5
    SLOPE0 = 0.2
    SLOPE1 = 0.01
    VS = 2048.0
    BITS = 16
    WPB = P // BITS
    ROW = D + 2
    DV = D + 1
    Q = 4
    QC = N // Q
    QB = QC // P
    XC = 8
    XB = 4
    LAG = 6
    UN = 8
    NPK = 4
    PKL = 3
    NX = 4
    SP0 = T // 2
    NS = T - SP0
    KW = 8
    KPB = P // KW
    NK = N // KW
    SLOTS = 24
    ROUNDS = 3

    pk_d = nc.dram_tensor("packed_adj", (T, P, T * WPB), u16).ap()
    x1_d = nc.dram_tensor("x_after_layer0", (T, P, D), f32).ap()
    h_d = nc.dram_tensor("h_of_layer1", (T, P, ROW), f32).ap()
    h1_d = nc.dram_tensor("h1_row", (T, P), f32).ap()

    x_v = x.rearrange("(t p) d -> p t d", p=P)
    adj_v = adj.rearrange("(t p) n -> t p n", p=P)
    out_v = out.rearrange("(t p) d -> p t d", p=P)

    outer = ExitStack()
    with outer:
        def psum(name):
            return outer.enter_context(nc.psum_tensor(name, [P, 512], f32))

        bank = [psum(f"bank{i}") for i in range(8)]
        h1all = outer.enter_context(nc.sbuf_tensor("h1all", [P, T], f32))
        h2all = outer.enter_context(nc.sbuf_tensor("h2all", [P, T], f32))
        cand = outer.enter_context(nc.sbuf_tensor("cand", [P, NS + 1, SLOTS], f32))
        cnt = outer.enter_context(nc.sbuf_tensor("cnt", [P, NS], f32))
        full = outer.enter_context(nc.sbuf_tensor("full", [P, 4], f32))
        idf = outer.enter_context(nc.sbuf_tensor("idf", [P, P], f32))

        ctx = ExitStack()
        with ctx:
            def sb(name, shape, dt):
                return ctx.enter_context(nc.sbuf_tensor(name, shape, dt))

            def sem(name):
                return ctx.enter_context(nc.semaphore(name))

            H = sb("H", [P, T, ROW], f32)
            V0 = H[:, :, :].bitcast(f16).rearrange("p t (s c) -> p t s c", s=2)
            adj_i = sb("adj_i", [P, Q, QC], i32)
            adj_f = sb("adj_f", [P, 2, N], f16)
            adjT = sb("adjT", [P, 2, T, P], u16)
            adjT_h = adjT[:, :, :, :].bitcast(f16)
            pk = sb("pk", [P, NPK, T * WPB], u16)
            packw = sb("packw", [P, WPB], f16)
            w_sb = sb("w_sb", [P, 2, D], f32)
            first = sb("first", [P, NK], f32)
            arow = first[:, 0:D]
            ubc = first[:, D:2 * D]
            ulhs = first[:, 2 * D:3 * D].rearrange("p (c n) -> p c n", c=2)
            a1row = sb("a1row", [P, 2, D], f32)
            ucol = sb("ucol", [P, 2], f32)
            st = sb("st", [P, XC, 6], f32)
            mv = sb("mv", [P, T, 2], f32)
            std = sb("std", [P, T], f32)
            rstd = sb("rstd", [P, T], f32)
            nmr = sb("nmr", [P, T], f32)
            r0 = sb("r0", [P, T], f32)
            rmax = sb("rmax", [P, 1], f32)
            Mb = sb("Mb", [P, 1], f32)
            nM = sb("nM", [P, 1], f32)
            p0 = sb("p0", [P, T], f32)
            p0s = sb("p0s", [P, T], f32)
            vtmp = sb("vtmp", [P, 4, ROW], f32)
            junk = sb("junk", [P, D], f32)
            eps = sb("eps", [P, 1], f32)
            xt = sb("xt", [P, NX, D], f32)
            x1 = sb("x1", [P, NX, D], f32)
            hh = sb("hh", [P, NX, ROW], f32)
            rden = sb("rden", [P, 1], f32)
            agg = sb("agg", [P, D], f32)
            aggT = sb("aggT", [P, 2, P], f32)
            ysb = sb("ysb", [P, D], f32)
            lr = sb("lr", [P, D], f32)
            st1 = sb("st1", [P, 6], f32)
            keyw = sb("keyw", [P, KPB], f16)
            keypos = sb("keypos", [P, NK], f16)
            kraw = vtmp[:, :, :].rearrange("p a b -> p (a b)")[:, 0:NK]
            ksg = first
            k24 = sb("k24", [P, UN, SLOTS], f32)
            ki = sb("ki", [P, UN, SLOTS], i32)
            kb = sb("kb", [P, UN, SLOTS], f32)
            c24 = kb
            kbase = k24
            khi = sb("khi", [P, UN, SLOTS], f32)
            kc = sb("kc", [P, UN, ROUNDS, SLOTS], f32)
            fl = sb("fl", [P, 4], f32)
            cnt8 = sb("cnt8", [P, UN], f32)
            fence = sb("fence", [P, 1], f32)
            mv1 = sb("mv1", [P, 2], f32)
            h12 = sb("h12", [P, 2], f32)
            std1 = sb("std1", [P, 1], f32)
            rstd1 = sb("rstd1", [P, 1], f32)
            nmr1 = sb("nmr1", [P, 1], f32)

            pkps = [bank[0], bank[1]]
            acc = [bank[2], bank[3]]
            tps, yps = bank[4], bank[5]
            ups = bank[6]
            kps = [bank[6], bank[7]]

            const_in = sem("const_in")
            x_in = [sem(f"x_in{i}") for i in range(XB)]
            adj_in = [sem(f"adj_in{i}") for i in range(Q)]
            xt_in = [sem(f"xt_in{i}") for i in range(NX)]
            ones_set = sem("ones_set")
            ucol_ready = sem("ucol_ready")
            ulhs_ready = sem("ulhs_ready")
            ups_ready = sem("ups_ready")
            ubc_ready = sem("ubc_ready")
            st_ready = sem("st_ready")
            mv_ready = sem("mv_ready")
            std_ready = sem("std_ready")
            rstd_ready = sem("rstd_ready")
            nmr_ready = sem("nmr_ready")
            h_ready = sem("h_ready")
            r_ready = sem("r_ready")
            rmax_ready = sem("rmax_ready")
            M_ready = sem("M_ready")
            nM_ready = sem("nM_ready")
            p0_ready = sem("p0_ready")
            p0s_ready = sem("p0s_ready")
            vtmp_ready = sem("vtmp_ready")
            vhi_ready = sem("vhi_ready")
            v0_ready = sem("v0_ready")
            conv_done = sem("conv_done")
            pack_done = sem("pack_done")
            pk_ready = sem("pk_ready")
            pk_out = [sem(f"pk_out{i}") for i in range(NPK)]
            adjT_ready = sem("adjT_ready")
            acc_ready = sem("acc_ready")
            rden_ready = sem("rden_ready")
            agg_ready = sem("agg_ready")
            tr_ready = sem("tr_ready")
            aggT_ready = sem("aggT_ready")
            y_ready = sem("y_ready")
            ysb_ready = sem("ysb_ready")
            lr_ready = sem("lr_ready")
            x1_ready = sem("x1_ready")
            st1_ready = sem("st1_ready")
            mv1_ready = sem("mv1_ready")
            std1_ready = sem("std1_ready")
            rstd1_ready = sem("rstd1_ready")
            nmr1_ready = sem("nmr1_ready")
            hh_ready = sem("hh_ready")
            h12_ready = sem("h12_ready")
            h12_kept = sem("h12_kept")
            keys_ps = sem("keys_ps")
            ksg_ready = sem("ksg_ready")
            kmul_ready = sem("kmul_ready")
            keys_ready = sem("keys_ready")
            top_ready = sem("top_ready")
            keys_used = sem("keys_used")
            dec_ready = sem("dec_ready")
            c24_ready = sem("c24_ready")
            x1_out = [sem(f"x1_out{i}") for i in range(NX)]
            hh_out = [sem(f"hh_out{i}") for i in range(NX)]

            block = ctx.enter_context(nc.Block())

            @block.sync
            def _(sp):
                sp.dma_start(w_sb[:, :, :], w0.rearrange("(c p) n -> p c n", p=P)).then_inc(const_in, 16)
                sp.dma_start(arow, a0[D:2 * D].rearrange("(o n) -> o n", o=1)
                             .partition_broadcast(P)).then_inc(const_in, 16)
                sp.dma_start(a1row[:, :, :], a1.rearrange("(o s n) b -> o s (n b)", o=1, s=2)
                             .partition_broadcast(P)).then_inc(const_in, 16)
                sp.dma_start(packw[:, :], pack_w).then_inc(const_in, 16)
                sp.dma_start(keyw[:, :], key_w).then_inc(const_in, 16)
                sp.dma_start(keypos[:, :], key_pos.rearrange("(o n) -> o n", o=1)
                             .partition_broadcast(P)).then_inc(const_in, 16)
                sp.dma_start(idf[:, :], ident).then_inc(const_in, 16)
                for c in range(T // XC):
                    if c >= XB:
                        sp.wait_ge(x_in[c % XB], c // XB * 16)
                    sp.dma_start(H[:, c * XC:(c + 1) * XC, 0:D],
                                 x_v[:, c * XC:(c + 1) * XC, :]).then_inc(x_in[c % XB], 16)

                def load(t, b, first):
                    for q in range(Q):
                        if not first:
                            sp.wait_ge(conv_done, t * Q - Q + q + 1)
                        sp.dma_start(adj_i[:, q, :], adj_v[bass.ds(t, 1), :, q * QC:(q + 1) * QC]
                                     .rearrange("o p n -> p (o n)")).then_inc(adj_in[q], 16)

                def load_x(t, b, first):
                    if not first:
                        sp.wait_ge(x1_ready, t - NX + 1)
                    sp.dma_start(xt[:, b, :], x_v[:, bass.ds(t, 1), :]
                                 .rearrange("p o d -> p (o d)")).then_inc(xt_in[b], 16)

                def store_words(t, pb):
                    sp.wait_ge(pk_ready, t + 1)
                    sp.dma_start(pk_d[bass.ds(t, 1), :, :].rearrange("o p n -> p (o n)"),
                                 pk[:, pb, :]).then_inc(pk_out[pb], 16)

                def store(t, b):
                    sp.wait_ge(x1_ready, t + 1)
                    sp.dma_start(x1_d[bass.ds(t, 1), :, :].rearrange("o p n -> p (o n)"),
                                 x1[:, b, :]).then_inc(x1_out[b], 16)
                    sp.wait_ge(h12_kept, 3 * t + 3)
                    sp.dma_start(h_d[bass.ds(t, 1), :, :].rearrange("o p n -> p (o n)"),
                                 hh[:, b, :]).then_inc(hh_out[b], 16)

                for t in range(UN):
                    load(t, t % NX, t == 0)
                    load_x(t, t % NX, t < NX)
                    if t >= PKL:
                        store_words(t - PKL, (t - PKL) % NPK)
                    if t >= LAG:
                        store(t - LAG, (t - LAG) % NX)
                with sp.Fori(1, T // UN) as k:
                    for j in range(UN):
                        t = k * UN + j
                        load(t, j % NX, False)
                        load_x(t, j % NX, False)
                        store_words(t - PKL, (j - PKL) % NPK)
                        store(t - LAG, (j - LAG) % NX)
                for t in range(T - PKL, T):
                    store_words(t, t % NPK)
                for t in range(T - LAG, T):
                    store(t, t % NX)
                for b in range(NPK):
                    sp.wait_ge(pk_out[b], 16 * (T // NPK))
                for b in range(NX):
                    sp.wait_ge(x1_out[b], 16 * (T // NX))
                    sp.wait_ge(hh_out[b], 16 * (T // NX))

            @block.gpsimd
            def _(pool):
                nc.gpsimd.memset(hh[:, :, D:ROW], 1.0).then_inc(ones_set, 1)
                nc.gpsimd.memset(H[:, :, D:ROW], 1.0).then_inc(ones_set, 1)
                nc.gpsimd.memset(eps[:, :], EPS).then_inc(ones_set, 1)
                pool.wait_ge(rmax_ready, 1)
                nc.gpsimd.partition_all_reduce(Mb[:, :], rmax[:, :], P, RMAX).then_inc(M_ready, 1)
                with pool.Fori(0, NS) as m:
                    pool.wait_ge(ksg_ready, m * 4 + 4)
                    nc.gpsimd.tensor_tensor(ksg[:, :], ksg[:, :], keypos[:, :], ALU.mult)\
                        .then_inc(kmul_ready, 1)
                    pool.wait_ge(kmul_ready, m + 1)
                    nc.gpsimd.tensor_tensor(kraw, kraw, ksg[:, :], ALU.add).then_inc(keys_ready, 1)

            @block.scalar
            def _(act):
                act.wait_ge(ones_set, 3)
                for c in range(T // XC):
                    act.wait_ge(mv_ready, XC * (c + 1))
                    nc.scalar.activation(std[:, c * XC:(c + 1) * XC], mv[:, c * XC:(c + 1) * XC, 1],
                                         ACT.Sqrt, bias=eps[:, :]).then_inc(std_ready, 1)
                    act.wait_ge(nmr_ready, c + 1)
                    with act.Fori(c * XC, c * XC + XC) as t:
                        nc.scalar.activation(H[:, t, 0:D], H[:, t, 0:D], ACT.Relu,
                                             scale=rstd[:, bass.ds(t, 1)],
                                             bias=nmr[:, bass.ds(t, 1)]).then_inc(h_ready, 1)

                def convert(t, b, qs, first):
                    for q in qs:
                        act.wait_ge(adj_in[q], (t + 1) * 16)
                        if not first and q == qs[0]:
                            act.wait_ge(pack_done, t - 1)
                        nc.scalar.activation(adj_f[:, b, q * QC:(q + 1) * QC], adj_i[:, q, :],
                                             ACT.Copy).then_inc(conv_done, 1)

                convert(0, 0, range(Q), True)
                act.wait_ge(nM_ready, 1)
                nc.scalar.activation(p0[:, :], r0[:, :], ACT.Exp, bias=nM[:, :]).then_inc(p0_ready, 1)
                act.wait_ge(p0s_ready, 1)
                def weigh(t, j, first):
                    if not first:
                        act.wait_ge(v0_ready, t - 3)
                    nc.scalar.activation(vtmp[:, j, :], H[:, t, :], ACT.Copy,
                                         scale=p0s[:, bass.ds(t, 1)]).then_inc(vtmp_ready, 1)

                for t in range(4):
                    weigh(t, t, True)
                with act.Fori(1, T // 4) as k:
                    for j in range(4):
                        weigh(k * 4 + j, j, False)
                convert(1, 1, range(Q), True)

                def finish(t, b):
                    act.wait_ge(y_ready, t + 1)
                    nc.scalar.activation(ysb[:, :], yps[:, 0:D], ACT.Copy).then_inc(ysb_ready, 1)
                    act.wait_ge(mv1_ready, t + 1)
                    nc.scalar.activation(std1[:, :], mv1[:, 1:2], ACT.Sqrt, bias=eps[:, :])\
                        .then_inc(std1_ready, 1)
                    act.wait_ge(nmr1_ready, t + 1)
                    nc.scalar.activation(hh[:, b, 0:D], x1[:, b, :], ACT.Relu, scale=rstd1[:, :],
                                         bias=nmr1[:, :]).then_inc(hh_ready, 1)

                def copy_aggT(t):
                    act.wait_ge(tr_ready, t + 1)
                    nc.scalar.activation(aggT[:, :, :].rearrange("p c n -> p (c n)"), tps[:, 0:D],
                                         ACT.Copy).then_inc(aggT_ready, 1)

                def copy_keys(t, first=False):
                    act.wait_ge(keys_ps, t - SP0 + 1)
                    if not first:
                        act.wait_ge(keys_used, t - SP0)
                    for i in range(2):
                        half = slice(i * NK // 2, (i + 1) * NK // 2)
                        nc.scalar.activation(kraw[:, half], kps[i][:, :], ACT.Copy,
                                             scale=1.0 / (1 << KW)).then_inc(ksg_ready, 1)
                        nc.scalar.activation(ksg[:, half], kps[i][:, :], ACT.Sign).then_inc(ksg_ready, 1)

                def step(t, j, reuse, t_has_tail=True):
                    convert(t + 2, j % 2, range(0, Q // 2), False)
                    if t_has_tail:
                        copy_aggT(t - 1)
                    convert(t + 2, j % 2, range(Q // 2, Q), False)
                    if t_has_tail:
                        if reuse is not None:
                            act.wait_ge(hh_out[(j - 1) % NX], reuse)
                        finish(t - 1, (j - 1) % NX)

                step(0, 0, None, t_has_tail=False)
                for t in range(1, NX + 1):
                    step(t, t % NX, None)
                for t in range(NX + 1, 2 * NX):
                    step(t, t % NX, 16)
                with act.Fori(2, SP0 // NX) as k:
                    for j in range(NX):
                        step(k * NX + j, j, k * 16 - 16 if j == 0 else k * 16)
                for j in range(NX):
                    step(SP0 + j, j, SP0 // NX * 16 - (16 if j == 0 else 0))
                    copy_keys(SP0 + j, j == 0)
                with act.Fori(SP0 // NX + 1, T // NX - 1) as k:
                    for j in range(NX):
                        step(k * NX + j, j, k * 16 - 16 if j == 0 else k * 16)
                        copy_keys(k * NX + j)
                last = T // NX - 1
                for j in range(NX):
                    t = last * NX + j
                    if t + 2 < T:
                        step(t, j, 16 * (last - 1) if j == 0 else 16 * last)
                    else:
                        copy_aggT(t - 1)
                        act.wait_ge(hh_out[(j - 1) % NX], 16 * last)
                        finish(t - 1, (j - 1) % NX)
                    copy_keys(t)
                copy_aggT(T - 1)
                act.wait_ge(hh_out[NX - 1], 16 * last)
                finish(T - 1, NX - 1)

            @block.vector
            def _(dve):
                dve.wait_ge(const_in, 16 * 7)
                for c in range(2):
                    nc.vector.tensor_tensor_reduce(out=junk[:, :], in0=w_sb[:, c, :], in1=arow,
                                                   scale=1.0, scalar=0.0, op0=ALU.mult, op1=ALU.add,
                                                   accum_out=ucol[:, c:c + 1]).then_inc(ucol_ready, 1)
                    dve.wait_ge(ucol_ready, c + 1)
                for c in range(2):
                    nc.vector.tensor_copy(ulhs[:, c, :], ucol[:, c:c + 1].to_broadcast([P, P]))\
                        .then_inc(ulhs_ready, 1)
                dve.wait_ge(ups_ready, 1)
                nc.vector.tensor_copy(ubc, ups[:, 0:D]).then_inc(ubc_ready, 1)
                dve.wait_ge(ubc_ready, 1)

                def dots(c):
                    for t in range(c * XC, c * XC + XC):
                        dve.wait_ge(h_ready, t + 1)
                        if t:
                            dve.wait_ge(r_ready, t)
                        nc.vector.tensor_tensor_reduce(out=junk[:, :], in0=H[:, t, 0:D], in1=ubc,
                                                       scale=1.0, scalar=0.0, op0=ALU.mult,
                                                       op1=ALU.add, accum_out=r0[:, t:t + 1])\
                            .then_inc(r_ready, 1)

                for c in range(T // XC):
                    cs = slice(c * XC, (c + 1) * XC)
                    dve.wait_ge(x_in[c % XB], 16 * (c // XB + 1))
                    for j in range(XC):
                        if c and j == 0:
                            dve.wait_ge(mv_ready, c * XC)
                        nc.vector.bn_stats(st[:, j, :], H[:, c * XC + j, 0:D]).then_inc(st_ready, 1)
                    for j in range(XC):
                        dve.wait_ge(st_ready, c * XC + j + 1)
                        nc.vector.bn_aggr(mv[:, c * XC + j, :], st[:, j, :]).then_inc(mv_ready, 1)
                    dve.wait_ge(std_ready, c + 1)
                    nc.vector.reciprocal(rstd[:, cs], std[:, cs]).then_inc(rstd_ready, 1)
                    dve.wait_ge(mv_ready, (c + 1) * XC)
                    dve.wait_ge(rstd_ready, c + 1)
                    nc.vector.scalar_tensor_tensor(nmr[:, cs], mv[:, cs, 0], -1.0, rstd[:, cs],
                                                   ALU.mult, ALU.mult).then_inc(nmr_ready, 1)
                    if c:
                        dots(c - 1)
                dots(T // XC - 1)
                dve.wait_ge(r_ready, T)
                nc.vector.reduce_max(rmax[:, :], r0[:, :], AX.X).then_inc(rmax_ready, 1)

                def take_packed(t, b, pb, reuse):
                    dve.wait_ge(pack_done, t + 1)
                    if reuse is not None:
                        dve.wait_ge(pk_out[pb], reuse)
                    nc.vector.tensor_copy(pk[:, pb, :], pkps[b][:, :]).then_inc(pk_ready, 1)
                    dve.wait_ge(pk_ready, t + 1)
                    words = pk[:, pb, :].rearrange("p (t w) -> p t w", w=WPB)
                    for k in range(BITS):
                        dst = adjT[:, b, :, k * WPB:(k + 1) * WPB]
                        if k <= 14:
                            i = nc.vector.tensor_scalar(dst, words, 1 << k, 14 - k, ALU.bitwise_and,
                                                        ALU.logical_shift_left)
                        else:
                            i = nc.vector.tensor_scalar(dst, words, 1 << k, k - 14, ALU.bitwise_and,
                                                        ALU.logical_shift_right)
                    i.then_inc(adjT_ready, 1)

                take_packed(0, 0, 0, None)
                nc.vector.memset(full[:, :], 0.0)
                nc.vector.memset(fl[:, :], 0.0)
                dve.wait_ge(M_ready, 1)
                nc.vector.tensor_scalar(nM[:, :], Mb[:, :], -1.0, None, ALU.mult).then_inc(nM_ready, 1)
                dve.wait_ge(p0_ready, 1)
                nc.vector.tensor_scalar(p0s[:, :], p0[:, :], VS, None, ALU.mult).then_inc(p0s_ready, 1)
                with dve.Fori(0, T // 4) as k:
                    for j in range(4):
                        t = k * 4 + j
                        dve.wait_ge(vtmp_ready, t + 1)
                        nc.vector.tensor_copy(V0[:, t, 0, :], vtmp[:, j, :]).then_inc(vhi_ready, 1)
                        dve.wait_ge(vhi_ready, t + 1)
                        nc.vector.tensor_tensor(V0[:, t, 1, :], vtmp[:, j, :], V0[:, t, 0, :],
                                                ALU.subtract).then_inc(v0_ready, 1)

                def normalise(t, b):
                    dve.wait_ge(acc_ready, t + 1)
                    nc.vector.reciprocal(rden[:, :], acc[b][:, D:DV]).then_inc(rden_ready, 1)
                    dve.wait_ge(rden_ready, t + 1)
                    nc.vector.tensor_scalar(agg[:, :], acc[b][:, 0:D], rden[:, :], None, ALU.mult)\
                        .then_inc(agg_ready, 1)

                def keep_dots(t, b):
                    nc.vector.tensor_copy(h1all[:, bass.ds(t, 1)], h12[:, 0:1]).then_inc(h12_kept, 1)
                    nc.vector.tensor_copy(h2all[:, bass.ds(t, 1)], h12[:, 1:2]).then_inc(h12_kept, 1)
                    nc.vector.tensor_copy(hh[:, b, DV:ROW], h12[:, 1:2]).then_inc(h12_kept, 1)

                def finish(t, b, n_in, reuse, kept):
                    dve.wait_ge(ysb_ready, t + 1)
                    nc.vector.scalar_tensor_tensor(lr[:, :], ysb[:, :], SLOPE0, ysb[:, :], ALU.mult,
                                                   ALU.max).then_inc(lr_ready, 1)
                    dve.wait_ge(lr_ready, t + 1)
                    dve.wait_ge(xt_in[b], n_in)
                    if reuse is not None:
                        dve.wait_ge(x1_out[b], reuse)
                    nc.vector.tensor_tensor(x1[:, b, :], lr[:, :], xt[:, b, :], ALU.add)\
                        .then_inc(x1_ready, 1)
                    dve.wait_ge(x1_ready, t + 1)
                    nc.vector.bn_stats(st1[:, :], x1[:, b, :]).then_inc(st1_ready, 1)
                    dve.wait_ge(st1_ready, t + 1)
                    if kept is not None:
                        keep_dots(t - 1, (b - 1) % NX)
                    nc.vector.bn_aggr(mv1[:, :], st1[:, :]).then_inc(mv1_ready, 1)
                    dve.wait_ge(std1_ready, t + 1)
                    nc.vector.reciprocal(rstd1[:, :], std1[:, :]).then_inc(rstd1_ready, 1)
                    dve.wait_ge(mv1_ready, t + 1)
                    dve.wait_ge(rstd1_ready, t + 1)
                    nc.vector.scalar_tensor_tensor(nmr1[:, :], mv1[:, 0:1], -1.0, rstd1[:, :],
                                                   ALU.mult, ALU.mult).then_inc(nmr1_ready, 1)
                    dve.wait_ge(hh_ready, t + 1)
                    if kept is not None:
                        dve.wait_ge(h12_kept, kept)
                    for s in range(2):
                        nc.vector.tensor_tensor_reduce(out=junk[:, :], in0=hh[:, b, 0:D],
                                                       in1=a1row[:, s, :], scale=1.0, scalar=0.0,
                                                       op0=ALU.mult, op1=ALU.add,
                                                       accum_out=h12[:, s:s + 1])\
                            .then_inc(h12_ready, 1)
                        dve.wait_ge(h12_ready, 2 * t + s + 1)

                def extract(t, j):
                    m = t - SP0
                    dve.wait_ge(keys_ready, m + 1)
                    nc.vector.memset(fence[:, :], 0.0)
                    for i in range(SLOTS // 8):
                        top = k24[:, j, 8 * i:8 * i + 8]
                        nc.vector.max(top, kraw).then_inc(top_ready, 1)
                        if i < SLOTS // 8 - 1:
                            dve.wait_ge(top_ready, m * 5 + 2 * i + 1)
                            nc.vector.memset(fence[:, :], 0.0)
                            nc.vector.match_replace(kraw, top, kraw, 0.0).then_inc(top_ready, 1)
                            dve.wait_ge(top_ready, m * 5 + 2 * i + 2)
                            nc.vector.memset(fence[:, :], 0.0)
                    dve.wait_ge(top_ready, m * 5 + 5)
                    nc.vector.memset(fence[:, :], 0.0).then_inc(keys_used, 1)

                def decode(e):
                    n = [0]
                    PER = 6 + 5 * ROUNDS - 1 + 6

                    def done(instruction):
                        n[0] += 1
                        instruction.then_inc(dec_ready, 1)
                        dve.wait_ge(dec_ready, e * PER + n[0])

                    k24v, kiv, kbv = k24[:, :, :], ki[:, :, :], kb[:, :, :]
                    done(nc.vector.reduce_max(fl[:, 1:2], k24[:, :, SLOTS - 1:SLOTS], AX.XY))
                    done(nc.vector.tensor_scalar(kiv, k24v, float(1 << KW), None, ALU.mult))
                    done(nc.vector.tensor_scalar(khi[:, :, :].bitcast(i32), kiv, 255, None,
                                                 ALU.bitwise_and))
                    done(nc.vector.tensor_copy(kbv, khi[:, :, :].bitcast(i32)))
                    done(nc.vector.tensor_scalar(kiv, kiv, 8, 3, ALU.logical_shift_right,
                                                 ALU.logical_shift_left))
                    done(nc.vector.tensor_scalar(kbase[:, :, :], kiv, -126.0, None, ALU.add))
                    for r in range(ROUNDS):
                        bits = kbv.bitcast(i32)
                        done(nc.vector.tensor_scalar(kiv, bits, 23, None, ALU.logical_shift_right))
                        done(nc.vector.tensor_tensor(khi[:, :, :], kiv, kbase[:, :, :], ALU.add))
                        done(nc.vector.scalar_tensor_tensor(kc[:, :, r, :], kbv, 0.0, khi[:, :, :],
                                                            ALU.is_gt, ALU.mult))
                        done(nc.vector.tensor_scalar(khi[:, :, :].bitcast(i32), bits, 0x7F800000,
                                                     None, ALU.bitwise_and))
                        if r < ROUNDS - 1:
                            done(nc.vector.tensor_tensor(kbv, kbv, khi[:, :, :], ALU.subtract))
                    done(nc.vector.tensor_tensor(khi[:, :, :], kbv, khi[:, :, :], ALU.subtract))
                    done(nc.vector.reduce_max(fl[:, 0:1], khi[:, :, :], AX.XY))
                    nc.vector.memset(fence[:, :], 0.0)
                    for j in range(UN):
                        words = kc[:, j, :, :]
                        for i in range(SLOTS // 8):
                            top = c24[:, j, 8 * i:8 * i + 8]
                            nc.vector.max(top, words).then_inc(c24_ready, 1)
                            if i < SLOTS // 8 - 1:
                                dve.wait_ge(c24_ready, (e * UN + j) * 5 + 2 * i + 1)
                                nc.vector.memset(fence[:, :], 0.0)
                                nc.vector.match_replace(words, top, words, 0.0).then_inc(c24_ready, 1)
                                dve.wait_ge(c24_ready, (e * UN + j) * 5 + 2 * i + 2)
                                nc.vector.memset(fence[:, :], 0.0)
                    dve.wait_ge(c24_ready, (e * UN + UN) * 5)
                    done(nc.vector.tensor_scalar(khi[:, :, :], c24[:, :, :], 0.0, None, ALU.is_gt))
                    done(nc.vector.reduce_max(fl[:, 2:3], c24[:, :, SLOTS - 1:SLOTS], AX.XY))
                    nc.vector.tensor_copy(cand[:, bass.ds(e * UN, UN), :], c24[:, :, :])
                    nc.vector.reduce_sum(cnt8[:, :], khi[:, :, :], AX.X).then_inc(dec_ready, 1)
                    dve.wait_ge(dec_ready, e * PER + PER - 1)
                    nc.vector.tensor_copy(cnt[:, bass.ds(e * UN, UN)], cnt8[:, :])
                    nc.vector.tensor_tensor(full[:, :], full[:, :], fl[:, :], ALU.max)\
                        .then_inc(dec_ready, 1)
                    dve.wait_ge(dec_ready, e * PER + PER)
                    assert n[0] == PER - 2, n[0]

                def step(t, j, pk_reuse, n_in, x1_reuse, kept, ahead=True, lists=False):
                    if n_in is not None:
                        normalise(t - 1, (j - 1) % 2)
                    if ahead:
                        take_packed(t + 1, (j + 1) % 2, (j + 1) % NPK, pk_reuse)
                    if lists:
                        extract(t - 1, (j - 1) % UN)
                    if n_in is not None:
                        finish(t - 1, (j - 1) % NX, n_in, x1_reuse, kept)

                def counts(t):
                    return (16 * ((t + 1) // NPK) or None, 16 * ((t - 1) // NX + 1),
                            16 * ((t - 1) // NX) or None, 3 * (t - 1) or None)

                step(0, 0, None, None, None, None)
                for t in range(1, UN):
                    step(t, t, *counts(t))
                def body(k, lists):
                    for j in range(UN):
                        done = (j - 1) // NX
                        step(k * UN + j, j, k * 32 + 16 * ((j + 1) // NPK),
                             k * 32 + 16 * (done + 1), k * 32 + 16 * done,
                             k * 3 * UN + 3 * (j - 1), lists=lists)
                        if lists and j == 0:
                            decode(k - SP0 // UN - 1)

                with dve.Fori(1, SP0 // UN) as k:
                    body(k, False)
                for j in range(UN):
                    t = SP0 + j
                    step(t, j, *counts(t), lists=j > 0)
                with dve.Fori(SP0 // UN + 1, T // UN - 1) as k:
                    body(k, True)
                for j in range(UN):
                    t = T - UN + j
                    step(t, j, *counts(t), ahead=t + 1 < T, lists=True)
                    if j == 0:
                        decode(NS // UN - 2)
                normalise(T - 1, 1)
                extract(T - 1, UN - 1)
                finish(T - 1, NX - 1, *counts(T)[1:])
                keep_dots(T - 1, NX - 1)
                decode(NS // UN - 1)

            @block.tensor
            def _(pe):
                pe.wait_ge(const_in, 16 * 7)
                pe.wait_ge(ulhs_ready, 2)
                for c in range(2):
                    last = nc.tensor.matmul(ups[:, c * P:(c + 1) * P], ulhs[:, c, :], idf[:, :],
                                            start=True, stop=True)
                last.then_inc(ups_ready, 1)

                def pack(t, b, first):
                    if not first:
                        pe.wait_ge(pk_ready, t - 1)
                    for q in range(Q):
                        pe.wait_ge(conv_done, t * Q + q + 1)
                        for jb in range(q * QB, (q + 1) * QB):
                            last = nc.tensor.matmul(pkps[b][:, jb * WPB:(jb + 1) * WPB],
                                                    adj_f[:, b, jb * P:(jb + 1) * P], packw[:, :],
                                                    start=True, stop=True)
                    last.then_inc(pack_done, 1)

                def keys(t, b):
                    pe.wait_ge(adjT_ready, t + 1)
                    if t is not SP0:
                        pe.wait_ge(ksg_ready, (t - SP0) * 4)
                    for jb in range(T):
                        at = jb * KPB % (NK // 2)
                        last = nc.tensor.matmul(kps[jb * KPB // (NK // 2)][:, at:at + KPB],
                                                adjT_h[:, b, jb, :], keyw[:, :],
                                                start=True, stop=True)
                    last.then_inc(keys_ps, 1)

                def transpose_agg(t):
                    pe.wait_ge(agg_ready, t + 1)
                    for c in range(2):
                        last = nc.tensor.transpose(tps[:, c * P:(c + 1) * P],
                                                   agg[:, c * P:(c + 1) * P], idf[:, :])
                    last.then_inc(tr_ready, 1)

                def project(t):
                    pe.wait_ge(aggT_ready, t + 1)
                    for c in range(2):
                        last = nc.tensor.matmul(yps[:, 0:D], aggT[:, c, :], w_sb[:, c, :],
                                                start=(c == 0), stop=(c == 1))
                    last.then_inc(y_ready, 1)

                def aggregate(t, b, v0_wait=False, reuse=True, tail=True):
                    pe.wait_ge(adjT_ready, t + 1)
                    if reuse:
                        pe.wait_ge(agg_ready, t - 1)
                    for jb in range(T):
                        if v0_wait:
                            pe.wait_ge(v0_ready, jb + 1)
                        for s in range(2):
                            last = nc.tensor.matmul(acc[b][:, 0:DV], adjT_h[:, b, jb, :],
                                                    V0[:, jb, s, 0:DV], start=(jb == 0 and s == 0),
                                                    stop=(jb == T - 1 and s == 1))
                        if tail and jb == T // 4:
                            transpose_agg(t - 1)
                        if tail and jb == 3 * T // 4:
                            project(t - 1)
                    last.then_inc(acc_ready, 1)

                pack(0, 0, True)
                pack(1, 1, True)
                aggregate(0, 0, v0_wait=True, reuse=False, tail=False)
                pack(2, 0, False)
                aggregate(1, 1, reuse=False)
                with pe.Fori(1, SP0 // 2) as k:
                    for b in range(2):
                        pack(k * 2 + b + 1, (b + 1) % 2, False)
                        aggregate(k * 2 + b, b)
                for b in range(2):
                    pack(SP0 + b + 1, (b + 1) % 2, False)
                    keys(SP0 + b, b)
                    aggregate(SP0 + b, b)
                with pe.Fori(SP0 // 2 + 1, T // 2 - 1) as k:
                    for b in range(2):
                        pack(k * 2 + b + 1, (b + 1) % 2, False)
                        keys(k * 2 + b, b)
                        aggregate(k * 2 + b, b)
                pack(T - 1, 1, False)
                keys(T - 2, 0)
                aggregate(T - 2, 0)
                keys(T - 1, 1)
                aggregate(T - 1, 1)
                transpose_agg(T - 1)
                project(T - 1)

        G = 4
        NG = T // G
        NGD = SP0 // G
        GC = G * P
        CB = 4
        NC = T // CB
        HS = 4
        GB = 8
        NB = SLOTS // GB
        GT = NS // NGD
        BIG = 2.0 ** 100
        SURE = 12
        STEP = 3
        CT = NC // GT
        assert CT == NB + 1
        LATE = 2
        ctx = ExitStack()
        with ctx:
            def sb(name, shape, dt):
                return ctx.enter_context(nc.sbuf_tensor(name, shape, dt))

            def sem(name):
                return ctx.enter_context(nc.semaphore(name))

            Vp = sb("Vp", [P, T, 2, ROW], f16)
            Vn = sb("Vn", [P, T, 2, ROW], f16)
            adjp = sb("adjp", [P, 2, CB, GC], u16)
            adjp_h = adjp[:, :, :, :].bitcast(f16)
            adjn = sb("adjn", [P, 2, CB, GC], u16)
            adjn_h = adjn[:, :, :, :].bitcast(f16)
            adjn_b = adjn[:, :, :, :].bitcast(bf16)
            pkg = sb("pkg", [P, 2, G, T * WPB], u16)
            h1bc = sb("h1bc", [P, 2, GC], f32)
            hs = sb("hs", [P, HS, ROW], f32)
            x1g = sb("x1g", [P, G, D], f32)
            evp = sb("evp", [P, G, DV], f32)
            evn = hs[:, :, 0:DV]
            gat = sb("gat", [P, NB, GB, ROW], f32)
            sacc = sb("sacc", [P, 2, DV], f32)
            x1s = sb("x1s", [P, 2, D], f32)
            ix = sb("ix", [P, 2, SLOTS], i32)
            e8 = sb("e8", [P, 2, 2, GB], f32)
            m8 = sb("m8", [P, GB], f32)
            w8 = sb("w8", [P, GB], f32)
            hb = sb("hb", [P, 2, T + 1], f32)
            hbt = sb("hbt", [P, 2, 2], f32)
            srd = sb("srd", [P, 1], f32)
            h1T = sb("h1T", [T, P], f32)
            M1 = sb("M1", [P, 4], f32)
            red_in = sb("red_in", [P, NS + 2], f32)
            red = sb("red", [P, NS + 2], f32)
            redi = sb("redi", [P, NS + 2], i32)
            pdum = sb("pdum", [P, 2], f32)
            E = sb("E", [P, 2, T], f32)
            Es = sb("Es", [P, 2, T], f32)
            nh2 = sb("nh2", [P, T], f32)
            sM = sb("sM", [P, 2, T], f32)
            tM = sb("tM", [P, T], f32)
            dM = sb("dM", [P, 2, T], f32)
            ab = sb("ab", [P, 2, T], f32)
            den2 = sb("den2", [P, 2, G], f32)
            den = sb("den", [P, G], f32)
            rd = sb("rd", [P, G], f32)
            fac = sb("fac", [P, 2, G], f32)

            h_in = [sem(f"h_in{i}") for i in range(HS)]
            pkg_in = [sem(f"pkg_in{i}") for i in range(2)]
            h1bc_in = [sem(f"h1bc_in{i}") for i in range(2)]
            x1g_in = sem("x1g_in")
            h1T_ps = sem("h1T_ps")
            h1T_sb = sem("h1T_sb")
            h1_out = sem("h1_out")
            mx_ready = sem("mx_ready")
            M_all = sem("M_all")
            redi_ready = sem("redi_ready")
            gat_zero = sem("gat_zero")
            nh2_ready = sem("nh2_ready")
            negM_ready = sem("negM_ready")
            E_ready = sem("E_ready")
            Es_ready = sem("Es_ready")
            sM_ready = sem("sM_ready")
            s01_ready = sem("s01_ready")
            tM_ready = sem("tM_ready")
            dM_ready = sem("dM_ready")
            ab_ready = sem("ab_ready")
            vhi1_ready = sem("vhi1_ready")
            v_ready = sem("v_ready")
            sign_ready = sem("sign_ready")
            bits_ready = sem("bits_ready")
            pos_ready = sem("pos_ready")
            neg_ready = sem("neg_ready")
            chunk_used = sem("chunk_used")
            evp_ready = sem("evp_ready")
            evn_ready = sem("evn_ready")
            den2_ready = sem("den2_ready")
            den_ready = sem("den_ready")
            rd_ready = sem("rd_ready")
            fac_ready = sem("fac_ready")
            on_ready = sem("on_ready")
            op_ready = sem("op_ready")
            o_ready = sem("o_ready")
            o_out = sem("o_out")
            ix_ready = sem("ix_ready")
            gathered = sem("gathered")
            pdum_done = sem("pdum_done")
            gat_in = [sem(f"gat_in{i}") for i in range(NB)]
            e8_ready = sem("e8_ready")
            m8_ready = sem("m8_ready")
            w8_ready = sem("w8_ready")
            hb_ready = sem("hb_ready")
            sacc_ready = sem("sacc_ready")
            row_added = sem("row_added")
            srd_ready = sem("srd_ready")
            so_ready = sem("so_ready")
            x1s_in = [sem(f"x1s_in{i}") for i in range(2)]
            so_out = [sem(f"so_out{i}") for i in range(2)]

            block = ctx.enter_context(nc.Block())

            @block.sync
            def _(sp):
                def load_words(g, b):
                    sp.dma_start(pkg[:, b, :, :], pk_d[bass.ds(g * G, G), :, :]
                                 .rearrange("g p n -> p g n")).then_inc(pkg_in[b], 16)

                def load_h1(g, b):
                    sp.dma_start(h1bc[:, b, :], h1_d[bass.ds(g * G, G), :]
                                 .rearrange("g p -> (g p)").rearrange("(o n) -> o n", o=1)
                                 .partition_broadcast(P)).then_inc(h1bc_in[b], 16)

                for b in range(HS):
                    sp.dma_start(hs[:, b, :], h_d[b]).then_inc(h_in[b], 16)
                load_words(0, 0)
                load_words(1, 1)
                sp.wait_ge(h1T_sb, 1)
                sp.dma_start(h1_d, h1T[:, :]).then_inc(h1_out, 16)
                sp.wait_ge(h1_out, 16)
                load_h1(0, 0)
                load_h1(1, 1)
                with sp.Fori(1, T // HS) as k:
                    for b in range(HS):
                        sp.wait_ge(v_ready, (k - 1) * (2 * HS) + 2 * b + 2)
                        sp.dma_start(hs[:, b, :], h_d[bass.ds(k * HS + b, 1), :, :]
                                     .rearrange("o p n -> p (o n)")).then_inc(h_in[b], 16)

                def group(g, b, ahead, first):
                    if not first:
                        sp.wait_ge(o_out, g * 16)
                    sp.dma_start(x1g[:, :, :], x1_d[bass.ds(g * G, G), :, :]
                                 .rearrange("g p n -> p g n")).then_inc(x1g_in, 16)
                    if ahead:
                        sp.wait_ge(bits_ready, g * NC + NC)
                        load_words(g + 2, b)
                        sp.wait_ge(sign_ready, g * NC + NC)
                        load_h1(g + 2, b)
                    sp.wait_ge(o_ready, g * G + G)
                    sp.dma_start(out_v[:, bass.ds(g * G, G), :], x1g[:, :, :]).then_inc(o_out, 16)

                group(0, 0, True, True)
                group(1, 1, True, False)
                with sp.Fori(1, NGD // 2 - 1) as k:
                    for b in range(2):
                        group(k * 2 + b, b, True, False)
                group(NGD - 2, 0, False, False)
                group(NGD - 1, 1, False, False)
                sp.wait_ge(o_out, NGD * 16)
                for b in range(2):
                    sp.wait_ge(so_out[b], NS // 2 * 16)
                with sp.If(sp.value_load(redi[0:1, NS + 1:NS + 2]) > 0):
                    load_words(NGD, 0)
                    load_words(NGD + 1, 1)
                    load_h1(NGD, 0)
                    load_h1(NGD + 1, 1)
                    with sp.Fori(NGD // 2, NG // 2 - 1) as k:
                        for b in range(2):
                            group(k * 2 + b, b, True, False)
                    group(NG - 2, 0, False, False)
                    group(NG - 1, 1, False, False)
                    sp.wait_ge(o_out, NG * 16)

            @block.gpsimd
            def _(pool):
                nc.gpsimd.memset(gat[:, :, :, :], 0.0).then_inc(gat_zero, 1)
                nc.gpsimd.memset(pdum[:, :], 0.0).then_inc(gat_zero, 1)
                pool.wait_ge(mx_ready, 1)
                nc.gpsimd.partition_all_reduce(red[:, :], red_in[:, :], P, RMAX).then_inc(M_all, 1)
                pool.wait_ge(redi_ready, 1)
                pool.wait_ge(gat_zero, 2)
                h_rows = h_d.rearrange("t p n -> (t p) n")
                fetched = [pool.alloc_register(f"fetched{r}") for r in range(NB)]
                for r in range(NB):
                    pool.reg_mov(fetched[r], 0)

                def batch_complete(r):
                    pool.wait_ge(gat_in[r], pool.snap(fetched[r]))
                    pool.sem_inc(gathered, 1)

                def gather_tile(m, b, first):
                    count = pool.value_load(redi[0:1, bass.ds(m, 1)])
                    for i in range(NB):
                        pool.wait_ge(ix_ready, m + 1)
                        if not first:
                            pool.wait_ge(row_added, (m - 1) * SLOTS + (i + 1) * GB)
                        if not first or i:
                            pool.wait_ge(pdum_done, m * NB + i)
                        nc.gpsimd.tensor_tensor(pdum[:, 0:1], pdum[:, 1:2], pdum[:, 1:2], ALU.mult)\
                            .then_inc(pdum_done, 1)

                        def fetch(slots):
                            for s in slots:
                                pool.indirect_dma_start(
                                    gat[:, i, s - i * GB, :], None, h_rows,
                                    bass.IndirectOffsetOnAxis(ap=ix[:, b, s:s + 1], axis=0))\
                                    .then_inc(gat_in[i], 16)
                            pool.reg_add(fetched[i], fetched[i], 16 * len(slots))

                        def fetch_if(s0, s1):
                            with pool.If(count > s0):
                                fetch(range(s0, s1))

                        s = i * GB
                        end = s + GB
                        told = first and i == 0
                        while s < end:
                            if s < SURE:
                                e = min(end, SURE, s + STEP)
                                fetch(range(s, e))
                            else:
                                e = min(end, s + STEP - (s - SURE) % STEP)
                                fetch_if(s, e)
                            s = e
                            if not told:
                                batch_complete((i - 1) % NB)
                                told = True

                gather_tile(0, 0, True)
                gather_tile(1, 1, False)
                with pool.Fori(1, NS // 2) as k:
                    for b in range(2):
                        gather_tile(k * 2 + b, b, False)
                batch_complete(NB - 1)

            @block.scalar
            def _(act):
                for b in range(2):
                    act.dma_start(x1s[:, b, :], x1_d[SP0 + b]).then_inc(x1s_in[b], 16)
                act.wait_ge(negM_ready, 2)
                nc.scalar.activation(E[:, 0, :], h2all[:, :], ACT.Exp, bias=M1[:, 2:3])\
                    .then_inc(E_ready, 1)
                nc.scalar.activation(E[:, 1, :], h2all[:, :], ACT.Exp, scale=SLOPE1, bias=M1[:, 3:4])\
                    .then_inc(E_ready, 1)
                act.wait_ge(dM_ready, 2)
                nc.scalar.activation(ab[:, :, :], dM[:, :, :], ACT.Exp).then_inc(ab_ready, 1)
                act.wait_ge(Es_ready, 1)

                def high_halves(t, j, n_in):
                    act.wait_ge(h_in[j], n_in)
                    for s, V in ((0, Vp), (1, Vn)):
                        nc.scalar.activation(V[:, t, 0, :], hs[:, j, :], ACT.Copy,
                                             scale=Es[:, s, t:t + 1]).then_inc(vhi1_ready, 1)

                def signs(n, b, g2, c, reuse):
                    if reuse:
                        act.wait_ge(chunk_used, n - 1)
                    for jb in range(CB):
                        j = c * CB + jb
                        i = nc.scalar.activation(adjn_b[:, b, jb, :], h1bc[:, g2, :], ACT.Relu,
                                                 scale=-BIG, bias=nh2[:, j:j + 1])
                    i.then_inc(sign_ready, 1)

                def sums(g, first):
                    act.wait_ge(chunk_used, g * NC + NC)
                    if not first:
                        act.wait_ge(op_ready, g * G)
                    for i in range(G):
                        nc.scalar.activation(evn[:, i, :], bank[2 * i + 1][:, 0:DV], ACT.Copy)\
                            .then_inc(evn_ready, 1)

                def scale_sums(g):
                    act.wait_ge(fac_ready, g * 2 + 2)
                    act.wait_ge(evn_ready, g * G + G)
                    for i in range(G):
                        nc.scalar.activation(evn[:, i, 0:D], evn[:, i, 0:D], ACT.Copy,
                                             scale=fac[:, 1, i:i + 1]).then_inc(on_ready, 1)

                def weights(q, i):
                    act.wait_ge(gathered, q + 1)
                    if q is not 0 and q is not 1:
                        act.wait_ge(m8_ready, q - 1)
                    for k, scale in ((0, 1.0), (1, SLOPE1)):
                        nc.scalar.activation(e8[:, i % 2, k, :], gat[:, i % NB, :, DV], ACT.Exp, scale=scale,
                                             bias=hbt[:, i // NB % 2, k:k + 1]).then_inc(e8_ready, 1)

                def tile_out(m, b, fill=True):
                    act.wait_ge(so_ready, m + 1)
                    act.dma_start(out_v[:, bass.ds(m + SP0, 1), :].rearrange("p o n -> p (o n)"),
                                  x1s[:, b, :]).then_inc(so_out[b], 16)
                    if fill:
                        act.wait_ge(so_out[1 - b], (m - 1 - (1 - b)) * 8 + 16)
                        act.dma_start(x1s[:, 1 - b, :], x1_d[bass.ds(m + SP0 + 1, 1), :, :]
                                      .rearrange("o p n -> p (o n)")).then_inc(x1s_in[1 - b], 16)

                def group(g, g2, next_in, first=False):
                    if first:
                        signs(0, 0, 0, 0, False)
                    for c in range(NC):
                        if first:
                            for j in range(CB):
                                high_halves(c * CB + j, j % HS, (c * CB + j) // HS * 16 + 16)
                        if c % CT:
                            k = c // CT * NB + c % CT - 1
                            weights(k if first else g * (GT * NB) + k, k)
                        if c < NC - 1:
                            signs(g * NC + c + 1, (c + 1) % 2, g2, c + 1, not first or c >= 1)
                        if c == 1 and not first:
                            scale_sums(g - 1)
                        if c % CT == 0 and (c or not first):
                            t = c // CT - 1
                            tile_out(g * GT + t, t % 2, not (first and t == 0))
                    if next_in is not None:
                        act.wait_ge(h1bc_in[1 - g2], next_in)
                        signs(g * NC + NC, 0, 1 - g2, 0, True)
                    sums(g, first)

                act.wait_ge(nh2_ready, 1)
                act.wait_ge(h1bc_in[0], 16)
                group(0, 0, 16, first=True)
                group(1, 1, 32)
                with act.Fori(1, NGD // 2 - 1) as k:
                    group(k * 2, 0, k * 16 + 16)
                    group(k * 2 + 1, 1, k * 16 + 32)
                group(NGD - 2, 0, NGD // 2 * 16)
                group(NGD - 1, 1, None)
                tile_out(NS - 1, 1, False)
                scale_sums(NGD - 1)
                with act.If(act.value_load(redi[0:1, NS + 1:NS + 2]) > 0):
                    def dense(g, g2, n_in, tail):
                        act.wait_ge(h1bc_in[g2], n_in)
                        for c in range(NC):
                            signs(g * NC + c, c % 2, g2, c, True)
                            if c == 1 and tail:
                                scale_sums(g - 1)
                        sums(g, False)

                    dense(NGD, 0, NGD * 8 + 16, False)
                    dense(NGD + 1, 1, NGD * 8 + 16, True)
                    with act.Fori(NGD // 2 + 1, NG // 2) as k:
                        for b in range(2):
                            dense(k * 2 + b, b, k * 16 + 16, True)
                    scale_sums(NG - 1)

            @block.vector
            def _(dve):
                nc.vector.tensor_copy(red_in[:, 0:NS], cnt[:, :])
                nc.vector.reduce_max(red_in[:, NS:NS + 1], h2all[:, :], AX.X)
                nc.vector.reduce_max(red_in[:, NS + 1:NS + 2], full[:, :], AX.X).then_inc(mx_ready, 1)
                dve.wait_ge(h1T_ps, 1)
                nc.vector.tensor_copy(h1T[:, :], bank[7][0:T, 0:P]).then_inc(h1T_sb, 1)
                nc.vector.tensor_scalar(nh2[:, :], h2all[:, :], -BIG, None, ALU.mult)\
                    .then_inc(nh2_ready, 1)
                def indices(m, b):
                    nc.vector.tensor_copy(hbt[:, b, :], hb[:, :, bass.ds(m + SP0, 1)]
                                          .rearrange("p k o -> p (k o)"))
                    nc.vector.tensor_scalar(ix[:, b, :], cand[:, bass.ds(m, 1), :]
                                            .rearrange("p o s -> p (o s)"), -1.0, 0.0, ALU.add,
                                            ALU.max).then_inc(ix_ready, 1)

                nc.vector.memset(cand[:, NS:NS + 1, :], 0.0)
                nc.vector.memset(hb[:, :, T:T + 1], 0.0)
                dve.wait_ge(M_all, 1)
                nc.vector.tensor_copy(redi[:, 0:NS], red[:, 0:NS])
                nc.vector.tensor_scalar(redi[:, NS + 1:NS + 2], red[:, NS + 1:NS + 2], 0.0, None,
                                        ALU.is_gt).then_inc(redi_ready, 1)
                Mh = red[:, NS:NS + 1]
                nc.vector.tensor_scalar(M1[:, 2:3], Mh, -1.0, None, ALU.mult).then_inc(negM_ready, 1)
                nc.vector.tensor_scalar(M1[:, 3:4], Mh, -SLOPE1, None, ALU.mult)\
                    .then_inc(negM_ready, 1)
                dve.wait_ge(negM_ready, 2)
                nc.vector.tensor_scalar(sM[:, 0, :], h1all[:, :], Mh, None, ALU.add)\
                    .then_inc(sM_ready, 1)
                dve.wait_ge(sM_ready, 1)
                nc.vector.tensor_scalar(sM[:, 1, :], sM[:, 0, :], SLOPE1, None, ALU.mult)\
                    .then_inc(s01_ready, 1)
                dve.wait_ge(s01_ready, 1)
                nc.vector.tensor_tensor(tM[:, :], sM[:, 0, :], sM[:, 1, :], ALU.max).then_inc(tM_ready, 1)
                dve.wait_ge(tM_ready, 1)
                for s in range(2):
                    nc.vector.tensor_tensor(dM[:, s, :], sM[:, s, :], tM[:, :], ALU.subtract)\
                        .then_inc(dM_ready, 1)
                dve.wait_ge(dM_ready, 2)
                for s in range(2):
                    nc.vector.tensor_scalar(hb[:, s, 0:T], dM[:, s, :], M1[:, 2 + s:3 + s], None, ALU.add)\
                        .then_inc(hb_ready, 1)
                dve.wait_ge(hb_ready, 2)
                indices(0, 0)
                dve.wait_ge(E_ready, 2)
                nc.vector.tensor_scalar(Es[:, :, :], E[:, :, :], VS, None, ALU.mult).then_inc(Es_ready, 1)
                dve.wait_ge(Es_ready, 1)

                def low_halves(t, j):
                    for s, V in ((0, Vp), (1, Vn)):
                        dve.wait_ge(vhi1_ready, 2 * t + s + 1)
                        nc.vector.scalar_tensor_tensor(V[:, t, 1, :], hs[:, j, :],
                                                       Es[:, s, t:t + 1], V[:, t, 0, :],
                                                       ALU.mult, ALU.subtract).then_inc(v_ready, 1)

                def split_chunk(n, b, g2, c, reuse, between=()):
                    if reuse:
                        dve.wait_ge(chunk_used, n - 1)
                    words = pkg[:, g2, :, :].rearrange("p g (t w) -> p t g w", w=WPB)
                    for k in range(BITS):
                        dst = adjp[:, b, :, :].rearrange("p t (g i) -> p t g i", g=G)\
                            [:, :, :, k * WPB:(k + 1) * WPB]
                        src = words[:, c * CB:(c + 1) * CB, :, :]
                        if k <= 14:
                            i = nc.vector.tensor_scalar(dst, src, 1 << k, 14 - k, ALU.bitwise_and,
                                                        ALU.logical_shift_left)
                        else:
                            i = nc.vector.tensor_scalar(dst, src, 1 << k, k - 14, ALU.bitwise_and,
                                                        ALU.logical_shift_right)
                    i.then_inc(bits_ready, 1)
                    both = adjp[:, b, :, :].rearrange("p t i -> p (t i)")
                    part = adjn[:, b, :, :].rearrange("p t i -> p (t i)")
                    for step in between[:1]:
                        step()
                    dve.wait_ge(bits_ready, n + 1)
                    dve.wait_ge(sign_ready, n + 1)
                    nc.vector.tensor_tensor(part, both, part, ALU.bitwise_and).then_inc(neg_ready, 1)
                    for step in between[1:]:
                        step()
                    dve.wait_ge(neg_ready, n + 1)
                    nc.vector.tensor_tensor(both, both, part, ALU.bitwise_xor).then_inc(pos_ready, 1)

                def finish(g):
                    dve.wait_ge(chunk_used, g * NC + NC)
                    for i in range(G):
                        nc.vector.tensor_copy(evp[:, i, :], bank[2 * i][:, 0:DV]).then_inc(evp_ready, 1)
                    dve.wait_ge(evp_ready, g * G + G)
                    dve.wait_ge(evn_ready, g * G + G)
                    for s, ev in ((0, evp), (1, evn)):
                        nc.vector.tensor_tensor(den2[:, s, :], ab[:, s, bass.ds(g * G, G)],
                                                ev[:, :, D], ALU.mult).then_inc(den2_ready, 1)
                    dve.wait_ge(den2_ready, g * 2 + 2)
                    nc.vector.tensor_tensor(den[:, :], den2[:, 0, :], den2[:, 1, :], ALU.add)\
                        .then_inc(den_ready, 1)
                    dve.wait_ge(den_ready, g + 1)
                    nc.vector.reciprocal(rd[:, :], den[:, :]).then_inc(rd_ready, 1)
                    dve.wait_ge(rd_ready, g + 1)
                    for s in range(2):
                        nc.vector.tensor_tensor(fac[:, s, :], ab[:, s, bass.ds(g * G, G)], rd[:, :],
                                                ALU.mult).then_inc(fac_ready, 1)

                def finish_rows(g):
                    dve.wait_ge(fac_ready, g * 2 + 2)
                    for i in range(G):
                        dve.wait_ge(on_ready, g * G + i + 1)
                        nc.vector.scalar_tensor_tensor(evp[:, i, 0:D], evp[:, i, 0:D],
                                                       fac[:, 0, i:i + 1], evn[:, i, 0:D],
                                                       ALU.mult, ALU.add).then_inc(op_ready, 1)
                    dve.wait_ge(x1g_in, g * 16 + 16)
                    for i in range(G):
                        dve.wait_ge(op_ready, g * G + i + 1)
                        nc.vector.tensor_tensor(x1g[:, i, :], x1g[:, i, :], evp[:, i, 0:D], ALU.add)\
                            .then_inc(o_ready, 1)

                def batch_add(q, k, m):
                    i = k % NB
                    dve.wait_ge(e8_ready, 2 * q + 2)
                    nc.vector.tensor_tensor(m8[:, :], e8[:, k % 2, 0, :], e8[:, k % 2, 1, :],
                                            ALU.max).then_inc(m8_ready, 1)
                    dve.wait_ge(m8_ready, q + 1)
                    nc.vector.scalar_tensor_tensor(
                        w8[:, :], cand[:, bass.ds(m, 1), i * GB:(i + 1) * GB]
                        .rearrange("p o s -> p (o s)"), 0.0, m8[:, :], ALU.is_gt, ALU.mult)\
                        .then_inc(w8_ready, 1)
                    dve.wait_ge(w8_ready, q + 1)
                    for s in range(GB - LATE):
                        add_row(q, i, s)

                def add_row(q, i, s):
                    row, w, acc = gat[:, i, s, 0:DV], w8[:, s:s + 1], sacc[:, s % 2, :]
                    if i or s >= 2:
                        dve.wait_ge(row_added, q * GB + s - 1)
                        nc.vector.scalar_tensor_tensor(acc, row, w, acc, ALU.mult, ALU.add)\
                            .then_inc(row_added, 1)
                    else:
                        nc.vector.tensor_scalar(acc, row, w, None, ALU.mult).then_inc(row_added, 1)

                def tile_finish(m, b, n_in):
                    dve.wait_ge(row_added, m * SLOTS + SLOTS)
                    nc.vector.tensor_tensor(sacc[:, 0, :], sacc[:, 0, :], sacc[:, 1, :], ALU.add)\
                        .then_inc(sacc_ready, 1)
                    dve.wait_ge(sacc_ready, m + 1)
                    nc.vector.reciprocal(srd[:, :], sacc[:, 0, D:DV]).then_inc(srd_ready, 1)
                    dve.wait_ge(srd_ready, m + 1)
                    dve.wait_ge(x1s_in[b], n_in)
                    nc.vector.scalar_tensor_tensor(x1s[:, b, :], sacc[:, 0, 0:D], srd[:, :],
                                                   x1s[:, b, :], ALU.mult, ALU.add)\
                        .then_inc(so_ready, 1)

                def group(g, g2, n_in, first=False):
                    dve.wait_ge(pkg_in[g2], n_in)
                    for c in range(NC):
                        k = (c - 1) // CT * NB + (c - 1) % CT
                        late = []
                        if c % CT != 1 and (c or not first):
                            late = [lambda s=s: add_row(g * (GT * NB) + k - 1, (k - 1) % NB, s)
                                    for s in range(GB - LATE, GB)]
                        split_chunk(g * NC + c, c % 2, g2, c, not first or c >= 2, late)
                        if first:
                            for j in range(CB):
                                low_halves(c * CB + j, j % HS)
                        if c == 0 and not first:
                            finish(g - 1)
                        if c == CT and not first:
                            finish_rows(g - 1)
                        if c % CT:
                            m = g * GT + c // CT
                            if c % CT == 1:
                                indices(m + 1, (c // CT + 1) % 2)
                            batch_add(g * (GT * NB) + k, k, m)
                        elif c or not first:
                            m = g * GT + c // CT - 1
                            b = (c // CT - 1) % 2
                            tile_finish(m, b, (m - b) * 8 + 16)

                dve.wait_ge(ab_ready, 1)
                group(0, 0, 16, first=True)
                group(1, 1, 16)
                with dve.Fori(1, NGD // 2) as k:
                    for g2 in range(2):
                        group(k * 2 + g2, g2, k * 16 + 16)
                for s in range(GB - LATE, GB):
                    add_row(NS * NB - 1, NB - 1, s)
                tile_finish(NS - 1, 1, NS // 2 * 16)
                finish(NGD - 1)
                finish_rows(NGD - 1)
                with dve.If(dve.value_load(redi[0:1, NS + 1:NS + 2]) > 0):
                    def dense(g, g2, n_in, tail):
                        dve.wait_ge(pkg_in[g2], n_in)
                        for c in range(NC):
                            split_chunk(g * NC + c, c % 2, g2, c, True)
                            if c == 0 and tail:
                                finish(g - 1)
                            if c == 2 and tail:
                                finish_rows(g - 1)

                    dense(NGD, 0, NGD * 8 + 16, False)
                    dense(NGD + 1, 1, NGD * 8 + 16, True)
                    with dve.Fori(NGD // 2 + 1, NG // 2) as k:
                        for g2 in range(2):
                            dense(k * 2 + g2, g2, k * 16 + 16, True)
                    finish(NG - 1)
                    finish_rows(NG - 1)

            @block.tensor
            def _(pe):
                nc.tensor.transpose(bank[7][0:T, 0:P], h1all[:, :], idf[:, :]).then_inc(h1T_ps, 1)

                def group(g, first):
                    for c in range(NC):
                        n = g * NC + c
                        b = c % 2
                        pe.wait_ge(pos_ready, n + 1)
                        for jb in range(CB):
                            j = c * CB + jb
                            if first:
                                pe.wait_ge(v_ready, 2 * j + 2)
                            for i in range(G):
                                for part, (m, V) in enumerate(((adjp_h, Vp), (adjn_h, Vn))):
                                    if j == 0:
                                        if first and i == 0 and part == 0:
                                            pe.wait_ge(h1T_sb, 1)
                                        if not first:
                                            pe.wait_ge(evn_ready if part else evp_ready,
                                                       g * G - G + i + 1)
                                    for s in range(2):
                                        last = nc.tensor.matmul(
                                            bank[2 * i + part][:, 0:DV],
                                            m[:, b, jb, i * P:(i + 1) * P], V[:, j, s, 0:DV],
                                            start=(j == 0 and s == 0), stop=(j == T - 1 and s == 1))
                        last.then_inc(chunk_used, 1)

                group(0, True)
                with pe.Fori(1, NGD) as g:
                    group(g, False)
                pe.wait_ge(redi_ready, 1)
                with pe.If(pe.value_load(redi[0:1, NS + 1:NS + 2]) > 0):
                    with pe.Fori(NGD, NG) as g:
                        group(g, False)


_INS = ['x', 'adj', 'L0_gnn_W', 'L0_gnn_a', 'L1_gnn_a']


def kernel(**inputs):
    import numpy as np
    import concourse.bacc as bacc
    from concourse import mybir as _mybir
    from concourse.bass_utils import run_bass_kernel_spmd as run

    nc = bacc.Bacc("TRN2", target_bir_lowering=False, num_devices=1)
    arrays, args = {}, []

    def add(name, a):
        arrays[name] = a
        args.append(nc.dram_tensor(name, a.shape, _mybir.dt.from_np(a.dtype), kind="ExternalInput").ap())

    for name in _INS:
        add(f"in_{name}", np.ascontiguousarray(inputs[name]))
    rows = np.arange(128)
    pack_w = np.zeros((128, 8), np.float16)
    pack_w[rows, rows % 8] = 2.0 ** (rows // 8)
    add("pack_w", pack_w)
    key_w = np.zeros((128, 16), np.float16)
    key_w[rows, rows // 8] = 2.0 ** (rows % 8 - 1)
    add("key_w", key_w)
    add("key_pos", np.arange(inputs["x"].shape[0] // 8).astype(np.float16))
    add("ident", np.eye(128, dtype=np.float32))
    out = nc.dram_tensor("out", inputs["x"].shape, _mybir.dt.float32, kind="ExternalOutput").ap()
    two_layer_graph_attention(nc, *args, out)
    r = run(nc, [arrays], core_ids=[0])
    return r.results[0]["out"]
```

```python
import concourse.bass as bass
from concourse import mybir
from contextlib import ExitStack


def two_layer_graph_attention(nc, x, adj, w0, a0, a1, pack_w, key_w, key_pos, ident, out):
    f32, f16 = mybir.dt.float32, mybir.dt.float16
    bf16, u16, i32 = mybir.dt.bfloat16, mybir.dt.uint16, mybir.dt.int32
    ALU = mybir.AluOpType
    ACT = mybir.ActivationFunctionType
    AX = mybir.AxisListType
    RMAX = bass.bass_isa.ReduceOp.max

    P = 128
    N, D = x.shape
    T = N // P
    EPS = 1e-5
    SLOPE0 = 0.2
    SLOPE1 = 0.01
    VS = 2048.0
    BITS = 16
    WPB = P // BITS
    ROW = D + 2
    DV = D + 1
    Q = 4
    QC = N // Q
    QB = QC // P
    XC = 8
    XB = 4
    LAG = 6
    UN = 8
    VU = 16
    NPK = 4
    PKL = 3
    NX = 4
    SP0 = T // 2
    NS = T - SP0
    assert NS == SP0 and NS % UN == 0
    KW = 8
    KPB = P // KW
    NK = N // KW
    SLOTS = 24
    ROUNDS = 3

    pk_d = nc.dram_tensor("packed_adj", (T, P, T * WPB), u16).ap()
    x1_d = nc.dram_tensor("x_after_layer0", (T, P, D), f32).ap()
    h_d = nc.dram_tensor("h_of_layer1", (T, P, ROW), f32).ap()
    h1_d = nc.dram_tensor("h1_row", (T, P), f32).ap()

    x_v = x.rearrange("(t p) d -> p t d", p=P)
    adj_v = adj.rearrange("(t p) n -> t p n", p=P)
    out_v = out.rearrange("(t p) d -> p t d", p=P)

    outer = ExitStack()
    with outer:
        def psum(name):
            return outer.enter_context(nc.psum_tensor(name, [P, 512], f32))

        bank = [psum(f"bank{i}") for i in range(8)]
        h1all = outer.enter_context(nc.sbuf_tensor("h1all", [P, T], f32))
        h2all = outer.enter_context(nc.sbuf_tensor("h2all", [P, T], f32))
        cand = outer.enter_context(nc.sbuf_tensor("cand", [P, NS + 1, SLOTS], f32))
        cnt = outer.enter_context(nc.sbuf_tensor("cnt", [P, NS], f32))
        full = outer.enter_context(nc.sbuf_tensor("full", [P, 4], f32))
        idf = outer.enter_context(nc.sbuf_tensor("idf", [P, P], f32))

        ctx = ExitStack()
        with ctx:
            def sb(name, shape, dt):
                return ctx.enter_context(nc.sbuf_tensor(name, shape, dt))

            def sem(name):
                return ctx.enter_context(nc.semaphore(name))

            SH = 4
            HV = sb("HV", [P, T + SH, ROW], f32)
            H = HV[:, SH:T + SH, :]
            V0 = HV[:, 0:T, :].bitcast(f16).rearrange("p t (s c) -> p t s c", s=2)
            adj_i = sb("adj_i", [P, Q, QC], i32)
            adj_f = sb("adj_f", [P, 2, N], f16)
            adjT = sb("adjT", [P, 2, T, P], u16)
            adjT_h = adjT[:, :, :, :].bitcast(f16)
            pk = sb("pk", [P, NPK, T * WPB], u16)
            packw = sb("packw", [P, WPB], f16)
            w_sb = sb("w_sb", [P, 2, D], f32)
            first = sb("first", [P, NK], f32)
            arow = first[:, 0:D]
            ubc = first[:, D:2 * D]
            ulhs = first[:, 2 * D:3 * D].rearrange("p (c n) -> p c n", c=2)
            a1row = sb("a1row", [P, 2, D], f32)
            ucol = sb("ucol", [P, 2], f32)
            st = sb("st", [P, XC, 6], f32)
            mv = sb("mv", [P, T, 2], f32)
            std = sb("std", [P, T], f32)
            rstd = sb("rstd", [P, T], f32)
            nmr = sb("nmr", [P, T], f32)
            r0 = sb("r0", [P, T], f32)
            rmax = sb("rmax", [P, 1], f32)
            Mb = sb("Mb", [P, 1], f32)
            nM = sb("nM", [P, 1], f32)
            p0 = sb("p0", [P, T], f32)
            p0s = sb("p0s", [P, T], f32)
            junk = sb("junk", [P, D], f32)
            eps = sb("eps", [P, 1], f32)
            xt = sb("xt", [P, NX, D], f32)
            x1 = sb("x1", [P, NX, D], f32)
            hh = sb("hh", [P, NX, ROW], f32)
            rden = sb("rden", [P, 1], f32)
            agg = sb("agg", [P, D], f32)
            aggT = sb("aggT", [P, 2, P], f32)
            ysb = sb("ysb", [P, D], f32)
            lr = sb("lr", [P, D], f32)
            st1 = sb("st1", [P, 6], f32)
            keyw = sb("keyw", [P, KPB], f16)
            keypos = sb("keypos", [P, NK], f16)
            kraw = HV[:, T:T + SH, :].rearrange("p a b -> p (a b)")[:, 0:NK]
            ksg = first
            k24 = sb("k24", [P, UN, SLOTS], f32)
            ki = sb("ki", [P, UN, SLOTS], i32)
            kb = sb("kb", [P, UN, SLOTS], f32)
            c24 = kb
            kbase = k24
            khi = sb("khi", [P, UN, SLOTS], f32)
            kc = sb("kc", [P, UN, ROUNDS, SLOTS], f32)
            fl = sb("fl", [P, 4], f32)
            cnt8 = sb("cnt8", [P, UN], f32)
            fence = sb("fence", [P, 2], f32)
            mv1 = sb("mv1", [P, 2], f32)
            h12 = sb("h12", [P, 2], f32)
            std1 = sb("std1", [P, 1], f32)
            rstd1 = sb("rstd1", [P, 1], f32)
            nmr1 = sb("nmr1", [P, 1], f32)

            pkps = [bank[0], bank[1]]
            acc = [bank[2], bank[3]]
            tps, yps = bank[4], bank[5]
            ups = bank[6]
            kps = [bank[6], bank[7]]

            const_in = sem("const_in")
            x_in = [sem(f"x_in{i}") for i in range(XB)]
            adj_in = [sem(f"adj_in{i}") for i in range(Q)]
            xt_in = [sem(f"xt_in{i}") for i in range(NX)]
            ones_set = sem("ones_set")
            ucol_ready = sem("ucol_ready")
            ulhs_ready = sem("ulhs_ready")
            ups_ready = sem("ups_ready")
            ubc_ready = sem("ubc_ready")
            st_ready = sem("st_ready")
            mv_ready = sem("mv_ready")
            std_ready = sem("std_ready")
            rstd_ready = sem("rstd_ready")
            nmr_ready = sem("nmr_ready")
            h_ready = sem("h_ready")
            r_ready = sem("r_ready")
            rmax_ready = sem("rmax_ready")
            M_ready = sem("M_ready")
            nM_ready = sem("nM_ready")
            p0_ready = sem("p0_ready")
            p0s_ready = sem("p0s_ready")
            vhi_ready = sem("vhi_ready")
            v0_ready = sem("v0_ready")
            conv_done = sem("conv_done")
            pack_done = sem("pack_done")
            pk_ready = sem("pk_ready")
            pk_out = [sem(f"pk_out{i}") for i in range(NPK)]
            adjT_ready = sem("adjT_ready")
            acc_ready = sem("acc_ready")
            rden_ready = sem("rden_ready")
            agg_ready = sem("agg_ready")
            tr_ready = sem("tr_ready")
            aggT_ready = sem("aggT_ready")
            y_ready = sem("y_ready")
            ysb_ready = sem("ysb_ready")
            lr_ready = sem("lr_ready")
            x1_ready = sem("x1_ready")
            st1_ready = sem("st1_ready")
            mv1_ready = sem("mv1_ready")
            std1_ready = sem("std1_ready")
            rstd1_ready = sem("rstd1_ready")
            nmr1_ready = sem("nmr1_ready")
            hh_ready = sem("hh_ready")
            h12_ready = sem("h12_ready")
            h12_kept = sem("h12_kept")
            keys_ps = sem("keys_ps")
            ksg_ready = sem("ksg_ready")
            kmul_ready = sem("kmul_ready")
            keys_ready = sem("keys_ready")
            top_ready = sem("top_ready")
            keys_used = sem("keys_used")
            dec_ready = sem("dec_ready")
            c24_ready = sem("c24_ready")
            x1_out = [sem(f"x1_out{i}") for i in range(NX)]
            hh_out = [sem(f"hh_out{i}") for i in range(NX)]

            block = ctx.enter_context(nc.Block())

            SPARSE, DENSE = SP0, -NS

            def offset(t):
                return SPARSE if t < NS else DENSE

            @block.sync
            def _(sp):
                sp.dma_start(w_sb[:, :, :], w0.rearrange("(c p) n -> p c n", p=P)).then_inc(const_in, 16)
                sp.dma_start(arow, a0[D:2 * D].rearrange("(o n) -> o n", o=1)
                             .partition_broadcast(P)).then_inc(const_in, 16)
                sp.dma_start(a1row[:, :, :], a1.rearrange("(o s n) b -> o s (n b)", o=1, s=2)
                             .partition_broadcast(P)).then_inc(const_in, 16)
                sp.dma_start(packw[:, :], pack_w).then_inc(const_in, 16)
                sp.dma_start(keyw[:, :], key_w).then_inc(const_in, 16)
                sp.dma_start(keypos[:, :], key_pos.rearrange("(o n) -> o n", o=1)
                             .partition_broadcast(P)).then_inc(const_in, 16)
                sp.dma_start(idf[:, :], ident).then_inc(const_in, 16)
                for c in range(T // XC):
                    if c >= XB:
                        sp.wait_ge(x_in[c % XB], c // XB * 16)
                    sp.dma_start(H[:, c * XC:(c + 1) * XC, 0:D],
                                 x_v[:, c * XC:(c + 1) * XC, :]).then_inc(x_in[c % XB], 16)

                def load(t, off, first):
                    for q in range(Q):
                        if not first:
                            sp.wait_ge(conv_done, t * Q - Q + q + 1)
                        sp.dma_start(adj_i[:, q, :], adj_v[bass.ds(t + off, 1), :, q * QC:(q + 1) * QC]
                                     .rearrange("o p n -> p (o n)")).then_inc(adj_in[q], 16)

                def load_x(t, off, b, first):
                    if not first:
                        sp.wait_ge(x1_ready, t - NX + 1)
                    sp.dma_start(xt[:, b, :], x_v[:, bass.ds(t + off, 1), :]
                                 .rearrange("p o d -> p (o d)")).then_inc(xt_in[b], 16)

                def store_words(t, off, pb):
                    sp.wait_ge(pk_ready, t + 1)
                    sp.dma_start(pk_d[bass.ds(t + off, 1), :, :].rearrange("o p n -> p (o n)"),
                                 pk[:, pb, :]).then_inc(pk_out[pb], 16)

                def store(t, off, b):
                    sp.wait_ge(x1_ready, t + 1)
                    sp.dma_start(x1_d[bass.ds(t + off, 1), :, :].rearrange("o p n -> p (o n)"),
                                 x1[:, b, :]).then_inc(x1_out[b], 16)
                    sp.wait_ge(h12_kept, 3 * t + 3)
                    sp.dma_start(h_d[bass.ds(t + off, 1), :, :].rearrange("o p n -> p (o n)"),
                                 hh[:, b, :]).then_inc(hh_out[b], 16)

                def whole(t):
                    load(t, offset(t), t == 0)
                    load_x(t, offset(t), t % NX, t < NX)
                    if t >= PKL:
                        store_words(t - PKL, offset(t - PKL), (t - PKL) % NPK)
                    if t >= LAG:
                        store(t - LAG, offset(t - LAG), (t - LAG) % NX)

                def steps(k, off):
                    for j in range(UN):
                        t = k * UN + j
                        load(t, off, False)
                        load_x(t, off, j % NX, False)
                        store_words(t - PKL, off, (j - PKL) % NPK)
                        store(t - LAG, off, (j - LAG) % NX)

                for t in range(UN):
                    whole(t)
                with sp.Fori(1, NS // UN) as k:
                    steps(k, SPARSE)
                for t in range(NS, NS + UN):
                    whole(t)
                with sp.Fori(NS // UN + 1, T // UN) as k:
                    steps(k, DENSE)
                for t in range(T - PKL, T):
                    store_words(t, DENSE, t % NPK)
                for t in range(T - LAG, T):
                    store(t, DENSE, t % NX)
                for b in range(NPK):
                    sp.wait_ge(pk_out[b], 16 * (T // NPK))
                for b in range(NX):
                    sp.wait_ge(x1_out[b], 16 * (T // NX))
                    sp.wait_ge(hh_out[b], 16 * (T // NX))

            @block.gpsimd
            def _(pool):
                nc.gpsimd.memset(hh[:, :, D:ROW], 1.0).then_inc(ones_set, 1)
                nc.gpsimd.memset(HV[:, SH:T + SH, D:ROW], 1.0).then_inc(ones_set, 1)
                nc.gpsimd.memset(eps[:, :], EPS).then_inc(ones_set, 1)
                pool.wait_ge(rmax_ready, 1)
                nc.gpsimd.partition_all_reduce(Mb[:, :], rmax[:, :], P, RMAX).then_inc(M_ready, 1)
                with pool.Fori(0, NS) as m:
                    pool.wait_ge(ksg_ready, m * 4 + 4)
                    nc.gpsimd.tensor_tensor(ksg[:, :], ksg[:, :], keypos[:, :], ALU.mult)\
                        .then_inc(kmul_ready, 1)
                    pool.wait_ge(kmul_ready, m + 1)
                    nc.gpsimd.tensor_tensor(kraw, kraw, ksg[:, :], ALU.add).then_inc(keys_ready, 1)

            @block.scalar
            def _(act):
                def convert(t, b, qs, first):
                    for q in qs:
                        act.wait_ge(adj_in[q], (t + 1) * 16)
                        if not first and q == qs[0]:
                            act.wait_ge(pack_done, t - 1)
                        nc.scalar.activation(adj_f[:, b, q * QC:(q + 1) * QC], adj_i[:, q, :],
                                             ACT.Copy).then_inc(conv_done, 1)

                def roots(c):
                    act.wait_ge(mv_ready, XC * (c + 1))
                    nc.scalar.activation(std[:, c * XC:(c + 1) * XC], mv[:, c * XC:(c + 1) * XC, 1],
                                         ACT.Sqrt, bias=eps[:, :]).then_inc(std_ready, 1)

                def relus(c):
                    act.wait_ge(nmr_ready, c + 1)
                    with act.Fori(c * 2, c * 2 + 2) as k:
                        for j in range(XC // 2):
                            t = k * (XC // 2) + j
                            nc.scalar.activation(H[:, t, 0:D], H[:, t, 0:D], ACT.Relu,
                                                 scale=rstd[:, bass.ds(t, 1)],
                                                 bias=nmr[:, bass.ds(t, 1)]).then_inc(h_ready, 1)

                act.wait_ge(ones_set, 3)
                roots(0)
                for c in range(1, T // XC):
                    roots(c)
                    relus(c - 1)
                    if c >= T // XC - Q + 1:
                        convert(0, 0, [c - (T // XC - Q + 1)], True)
                relus(T // XC - 1)
                convert(0, 0, [Q - 1], True)
                convert(1, 1, range(Q), True)
                act.wait_ge(nM_ready, 1)
                nc.scalar.activation(p0[:, :], r0[:, :], ACT.Exp, bias=nM[:, :]).then_inc(p0_ready, 1)
                act.wait_ge(p0s_ready, 1)

                def weigh(t, first):
                    if not first:
                        act.wait_ge(v0_ready, t - SH + 1)
                    nc.scalar.activation(V0[:, t, 0, :], H[:, t, :], ACT.Copy,
                                         scale=p0s[:, bass.ds(t, 1)]).then_inc(vhi_ready, 1)

                for t in range(SH):
                    weigh(t, True)
                for t in range(SH, VU):
                    weigh(t, False)
                with act.Fori(1, T // VU) as k:
                    for j in range(VU):
                        weigh(k * VU + j, False)

                def finish(t, b):
                    act.wait_ge(y_ready, t + 1)
                    nc.scalar.activation(ysb[:, :], yps[:, 0:D], ACT.Copy).then_inc(ysb_ready, 1)
                    act.wait_ge(mv1_ready, t + 1)
                    nc.scalar.activation(std1[:, :], mv1[:, 1:2], ACT.Sqrt, bias=eps[:, :])\
                        .then_inc(std1_ready, 1)
                    act.wait_ge(nmr1_ready, t + 1)
                    nc.scalar.activation(hh[:, b, 0:D], x1[:, b, :], ACT.Relu, scale=rstd1[:, :],
                                         bias=nmr1[:, :]).then_inc(hh_ready, 1)

                def copy_aggT(t):
                    act.wait_ge(tr_ready, t + 1)
                    nc.scalar.activation(aggT[:, :, :].rearrange("p c n -> p (c n)"), tps[:, 0:D],
                                         ACT.Copy).then_inc(aggT_ready, 1)

                def copy_keys(t, first=False):
                    act.wait_ge(keys_ps, t + 1)
                    if not first:
                        act.wait_ge(keys_used, t)
                    for i in range(2):
                        half = slice(i * NK // 2, (i + 1) * NK // 2)
                        nc.scalar.activation(kraw[:, half], kps[i][:, :], ACT.Copy,
                                             scale=1.0 / (1 << KW)).then_inc(ksg_ready, 1)
                        nc.scalar.activation(ksg[:, half], kps[i][:, :], ACT.Sign).then_inc(ksg_ready, 1)

                def step(t, j, reuse, t_has_tail=True, lists=False):
                    convert(t + 2, j % 2, range(0, Q // 2), False)
                    if t_has_tail:
                        copy_aggT(t - 1)
                    convert(t + 2, j % 2, range(Q // 2, Q), False)
                    if lists:
                        copy_keys(t)
                    if t_has_tail:
                        if reuse is not None:
                            act.wait_ge(hh_out[(j - 1) % NX], reuse)
                        finish(t - 1, (j - 1) % NX)

                act.wait_ge(v0_ready, T)
                copy_keys(0, True)
                step(0, 0, None, t_has_tail=False)
                for t in range(1, 2 * NX):
                    step(t, t % NX, 16 if t > NX else None, lists=True)
                with act.Fori(2, NS // NX) as k:
                    for j in range(NX):
                        step(k * NX + j, j, k * 16 - 16 if j == 0 else k * 16, lists=True)
                with act.Fori(NS // NX, T // NX - 1) as k:
                    for j in range(NX):
                        step(k * NX + j, j, k * 16 - 16 if j == 0 else k * 16)
                last = T // NX - 1
                for j in range(NX):
                    t = last * NX + j
                    if t + 2 < T:
                        step(t, j, 16 * (last - 1) if j == 0 else 16 * last)
                    else:
                        copy_aggT(t - 1)
                        act.wait_ge(hh_out[(j - 1) % NX], 16 * last)
                        finish(t - 1, (j - 1) % NX)
                copy_aggT(T - 1)
                act.wait_ge(hh_out[NX - 1], 16 * last)
                finish(T - 1, NX - 1)

            @block.vector
            def _(dve):
                dve.wait_ge(const_in, 16 * 7)
                for c in range(2):
                    nc.vector.tensor_tensor_reduce(out=junk[:, :], in0=w_sb[:, c, :], in1=arow,
                                                   scale=1.0, scalar=0.0, op0=ALU.mult, op1=ALU.add,
                                                   accum_out=ucol[:, c:c + 1]).then_inc(ucol_ready, 1)
                    dve.wait_ge(ucol_ready, c + 1)
                for c in range(2):
                    nc.vector.tensor_copy(ulhs[:, c, :], ucol[:, c:c + 1].to_broadcast([P, P]))\
                        .then_inc(ulhs_ready, 1)
                dve.wait_ge(ups_ready, 1)
                nc.vector.tensor_copy(ubc, ups[:, 0:D]).then_inc(ubc_ready, 1)
                dve.wait_ge(ubc_ready, 1)

                def dots(c):
                    for t in range(c * XC, c * XC + XC):
                        dve.wait_ge(h_ready, t + 1)
                        if t >= 2:
                            dve.wait_ge(r_ready, t - 1)
                        nc.vector.tensor_tensor_reduce(out=(junk, lr)[t % 2][:, :], in0=H[:, t, 0:D], in1=ubc,
                                                       scale=1.0, scalar=0.0, op0=ALU.mult,
                                                       op1=ALU.add, accum_out=r0[:, t:t + 1])\
                            .then_inc(r_ready, 1)

                def statistics(c):
                    dve.wait_ge(x_in[c % XB], 16 * (c // XB + 1))
                    for j in range(XC):
                        if c and j == 0:
                            dve.wait_ge(mv_ready, c * XC)
                        nc.vector.bn_stats(st[:, j, :], H[:, c * XC + j, 0:D]).then_inc(st_ready, 1)
                    for j in range(XC):
                        dve.wait_ge(st_ready, c * XC + j + 1)
                        nc.vector.bn_aggr(mv[:, c * XC + j, :], st[:, j, :]).then_inc(mv_ready, 1)

                def scales(c):
                    cs = slice(c * XC, (c + 1) * XC)
                    dve.wait_ge(std_ready, c + 1)
                    nc.vector.reciprocal(rstd[:, cs], std[:, cs]).then_inc(rstd_ready, 1)
                    dve.wait_ge(mv_ready, (c + 1) * XC)
                    dve.wait_ge(rstd_ready, c + 1)
                    nc.vector.scalar_tensor_tensor(nmr[:, cs], mv[:, cs, 0], -1.0, rstd[:, cs],
                                                   ALU.mult, ALU.mult).then_inc(nmr_ready, 1)

                for c in range(T // XC + 2):
                    if c < T // XC:
                        statistics(c)
                    if 1 <= c <= T // XC:
                        scales(c - 1)
                    if c >= 2:
                        dots(c - 2)
                dve.wait_ge(r_ready, T)
                nc.vector.reduce_max(rmax[:, :], r0[:, :], AX.X).then_inc(rmax_ready, 1)

                def take_packed(t, b, pb, reuse):
                    dve.wait_ge(pack_done, t + 1)
                    if reuse is not None:
                        dve.wait_ge(pk_out[pb], reuse)
                    nc.vector.tensor_copy(pk[:, pb, :], pkps[b][:, :]).then_inc(pk_ready, 1)
                    dve.wait_ge(pk_ready, t + 1)
                    words = pk[:, pb, :].rearrange("p (t w) -> p t w", w=WPB)
                    for k in range(BITS):
                        dst = adjT[:, b, :, k * WPB:(k + 1) * WPB]
                        if k <= 14:
                            i = nc.vector.tensor_scalar(dst, words, 1 << k, 14 - k, ALU.bitwise_and,
                                                        ALU.logical_shift_left)
                        else:
                            i = nc.vector.tensor_scalar(dst, words, 1 << k, k - 14, ALU.bitwise_and,
                                                        ALU.logical_shift_right)
                    i.then_inc(adjT_ready, 1)

                take_packed(0, 0, 0, None)
                nc.vector.memset(full[:, :], 0.0)
                nc.vector.memset(fl[:, :], 0.0)
                dve.wait_ge(M_ready, 1)
                nc.vector.tensor_scalar(nM[:, :], Mb[:, :], -1.0, None, ALU.mult).then_inc(nM_ready, 1)
                take_packed(1, 1, 1, None)
                dve.wait_ge(p0_ready, 1)
                nc.vector.tensor_scalar(p0s[:, :], p0[:, :], VS, None, ALU.mult).then_inc(p0s_ready, 1)
                with dve.Fori(0, T // VU) as k:
                    for j in range(VU):
                        t = k * VU + j
                        dve.wait_ge(vhi_ready, t + 1)
                        nc.vector.scalar_tensor_tensor(V0[:, t, 1, :], H[:, t, :],
                                                       p0s[:, bass.ds(t, 1)], V0[:, t, 0, :],
                                                       ALU.mult, ALU.subtract).then_inc(v0_ready, 1)

                def normalise(t, b):
                    dve.wait_ge(acc_ready, t + 1)
                    nc.vector.reciprocal(rden[:, :], acc[b][:, D:DV]).then_inc(rden_ready, 1)
                    dve.wait_ge(rden_ready, t + 1)
                    nc.vector.tensor_scalar(agg[:, :], acc[b][:, 0:D], rden[:, :], None, ALU.mult)\
                        .then_inc(agg_ready, 1)

                def keep_dots(t, off, b):
                    nc.vector.tensor_copy(h1all[:, bass.ds(t + off, 1)], h12[:, 0:1]).then_inc(h12_kept, 1)
                    nc.vector.tensor_copy(h2all[:, bass.ds(t + off, 1)], h12[:, 1:2]).then_inc(h12_kept, 1)
                    nc.vector.tensor_copy(hh[:, b, DV:ROW], h12[:, 1:2]).then_inc(h12_kept, 1)

                def finish(t, b, n_in, reuse, kept, off):
                    dve.wait_ge(ysb_ready, t + 1)
                    nc.vector.scalar_tensor_tensor(lr[:, :], ysb[:, :], SLOPE0, ysb[:, :], ALU.mult,
                                                   ALU.max).then_inc(lr_ready, 1)
                    dve.wait_ge(lr_ready, t + 1)
                    dve.wait_ge(xt_in[b], n_in)
                    if reuse is not None:
                        dve.wait_ge(x1_out[b], reuse)
                    nc.vector.tensor_tensor(x1[:, b, :], lr[:, :], xt[:, b, :], ALU.add)\
                        .then_inc(x1_ready, 1)
                    dve.wait_ge(x1_ready, t + 1)
                    nc.vector.bn_stats(st1[:, :], x1[:, b, :]).then_inc(st1_ready, 1)
                    dve.wait_ge(st1_ready, t + 1)
                    if kept is not None:
                        keep_dots(t - 1, off, (b - 1) % NX)
                    nc.vector.bn_aggr(mv1[:, :], st1[:, :]).then_inc(mv1_ready, 1)
                    dve.wait_ge(std1_ready, t + 1)
                    nc.vector.reciprocal(rstd1[:, :], std1[:, :]).then_inc(rstd1_ready, 1)
                    dve.wait_ge(mv1_ready, t + 1)
                    dve.wait_ge(rstd1_ready, t + 1)
                    nc.vector.scalar_tensor_tensor(nmr1[:, :], mv1[:, 0:1], -1.0, rstd1[:, :],
                                                   ALU.mult, ALU.mult).then_inc(nmr1_ready, 1)
                    dve.wait_ge(hh_ready, t + 1)
                    if kept is not None:
                        dve.wait_ge(h12_kept, kept)
                    for s in range(2):
                        nc.vector.tensor_tensor_reduce(out=junk[:, :], in0=hh[:, b, 0:D],
                                                       in1=a1row[:, s, :], scale=1.0, scalar=0.0,
                                                       op0=ALU.mult, op1=ALU.add,
                                                       accum_out=h12[:, s:s + 1])\
                            .then_inc(h12_ready, 1)
                        dve.wait_ge(h12_ready, 2 * t + s + 1)

                def extract(t, j):
                    dve.wait_ge(keys_ready, t + 1)
                    nc.vector.memset(fence[:, 0:1], 0.0)
                    for i in range(SLOTS // 8):
                        top = k24[:, j, 8 * i:8 * i + 8]
                        nc.vector.max(top, kraw).then_inc(top_ready, 1)
                        if i < SLOTS // 8 - 1:
                            dve.wait_ge(top_ready, t * 5 + 2 * i + 1)
                            nc.vector.memset(fence[:, 0:1], 0.0)
                            nc.vector.match_replace(kraw, top, kraw, 0.0).then_inc(top_ready, 1)
                            dve.wait_ge(top_ready, t * 5 + 2 * i + 2)
                            nc.vector.memset(fence[:, 0:1], 0.0)
                    dve.wait_ge(top_ready, t * 5 + 5)
                    nc.vector.memset(fence[:, 0:1], 0.0).then_inc(keys_used, 1)

                BITS_OPS = 6 + 5 * ROUNDS - 1 + 2
                PER = BITS_OPS + 4

                def decode_bits(e):
                    n = [0]

                    def done(instruction):
                        n[0] += 1
                        instruction.then_inc(dec_ready, 1)
                        dve.wait_ge(dec_ready, e * PER + n[0])

                    k24v, kiv, kbv = k24[:, :, :], ki[:, :, :], kb[:, :, :]
                    done(nc.vector.reduce_max(fl[:, 1:2], k24[:, :, SLOTS - 1:SLOTS], AX.XY))
                    done(nc.vector.tensor_scalar(kiv, k24v, float(1 << KW), None, ALU.mult))
                    done(nc.vector.tensor_scalar(khi[:, :, :].bitcast(i32), kiv, 255, None,
                                                 ALU.bitwise_and))
                    done(nc.vector.tensor_copy(kbv, khi[:, :, :].bitcast(i32)))
                    done(nc.vector.tensor_scalar(kiv, kiv, 8, 3, ALU.logical_shift_right,
                                                 ALU.logical_shift_left))
                    done(nc.vector.tensor_scalar(kbase[:, :, :], kiv, -126.0, None, ALU.add))
                    for r in range(ROUNDS):
                        bits = kbv.bitcast(i32)
                        done(nc.vector.tensor_scalar(kiv, bits, 23, None, ALU.logical_shift_right))
                        done(nc.vector.tensor_tensor(khi[:, :, :], kiv, kbase[:, :, :], ALU.add))
                        done(nc.vector.scalar_tensor_tensor(kc[:, :, r, :], kbv, 0.0, khi[:, :, :],
                                                            ALU.is_gt, ALU.mult))
                        done(nc.vector.tensor_scalar(khi[:, :, :].bitcast(i32), bits, 0x7F800000,
                                                     None, ALU.bitwise_and))
                        if r < ROUNDS - 1:
                            done(nc.vector.tensor_tensor(kbv, kbv, khi[:, :, :], ALU.subtract))
                    done(nc.vector.tensor_tensor(khi[:, :, :], kbv, khi[:, :, :], ALU.subtract))
                    done(nc.vector.reduce_max(fl[:, 0:1], khi[:, :, :], AX.XY))
                    assert n[0] == BITS_OPS, n[0]

                def decode_list(e, j):
                    nc.vector.memset(fence[:, 1:2], 0.0)
                    words = kc[:, j, :, :]
                    for i in range(SLOTS // 8):
                        top = c24[:, j, 8 * i:8 * i + 8]
                        nc.vector.max(top, words).then_inc(c24_ready, 1)
                        if i < SLOTS // 8 - 1:
                            dve.wait_ge(c24_ready, (e * UN + j) * 5 + 2 * i + 1)
                            nc.vector.memset(fence[:, 1:2], 0.0)
                            nc.vector.match_replace(words, top, words, 0.0).then_inc(c24_ready, 1)
                            dve.wait_ge(c24_ready, (e * UN + j) * 5 + 2 * i + 2)
                            nc.vector.memset(fence[:, 1:2], 0.0)

                def decode_end(e):
                    at = e * PER + BITS_OPS
                    dve.wait_ge(c24_ready, (e * UN + UN) * 5)
                    nc.vector.tensor_scalar(khi[:, :, :], c24[:, :, :], 0.0, None, ALU.is_gt)\
                        .then_inc(dec_ready, 1)
                    nc.vector.reduce_max(fl[:, 2:3], c24[:, :, SLOTS - 1:SLOTS], AX.XY)\
                        .then_inc(dec_ready, 1)
                    nc.vector.tensor_copy(cand[:, bass.ds(e * UN, UN), :], c24[:, :, :])
                    dve.wait_ge(dec_ready, at + 1)
                    nc.vector.reduce_sum(cnt8[:, :], khi[:, :, :], AX.X).then_inc(dec_ready, 1)
                    dve.wait_ge(dec_ready, at + 3)
                    nc.vector.tensor_copy(cnt[:, bass.ds(e * UN, UN)], cnt8[:, :])
                    nc.vector.tensor_tensor(full[:, :], full[:, :], fl[:, :], ALU.max)\
                        .then_inc(dec_ready, 1)
                    dve.wait_ge(dec_ready, at + 4)

                def decode(e, j):
                    if j == 0:
                        decode_bits(e)
                    decode_list(e, j)
                    if j == UN - 1:
                        decode_end(e)

                def step(t, j, pk_reuse, n_in, x1_reuse, kept, off, ahead=True, lists=False, e=None):
                    if n_in is not None:
                        normalise(t - 1, (j - 1) % 2)
                    if ahead:
                        take_packed(t + 1, (j + 1) % 2, (j + 1) % NPK, pk_reuse)
                    if lists:
                        extract(t - 1, (j - 1) % UN)
                    if e is not None:
                        decode(e, j)
                    if n_in is not None:
                        finish(t - 1, (j - 1) % NX, n_in, x1_reuse, kept, off)

                def counts(t):
                    return (16 * ((t + 1) // NPK) or None, 16 * ((t - 1) // NX + 1),
                            16 * ((t - 1) // NX) or None, 3 * (t - 1) or None, offset(t - 2))

                def body(k, off, lists):
                    for j in range(UN):
                        done = (j - 1) // NX
                        step(k * UN + j, j, k * 32 + 16 * ((j + 1) // NPK),
                             k * 32 + 16 * (done + 1), k * 32 + 16 * done,
                             k * 3 * UN + 3 * (j - 1), off, lists=lists,
                             e=k - 1 if lists else None)

                for t in range(1, UN):
                    step(t, t, *counts(t), lists=True)
                with dve.Fori(1, NS // UN) as k:
                    body(k, SPARSE, True)
                for j in range(UN):
                    step(NS + j, j, *counts(NS + j), lists=j == 0, e=NS // UN - 1)
                with dve.Fori(NS // UN + 1, T // UN - 1) as k:
                    body(k, DENSE, False)
                for j in range(UN):
                    t = T - UN + j
                    step(t, j, *counts(t), ahead=t + 1 < T)
                normalise(T - 1, 1)
                finish(T - 1, NX - 1, *counts(T)[1:])
                keep_dots(T - 1, DENSE, NX - 1)

            @block.tensor
            def _(pe):
                pe.wait_ge(const_in, 16 * 7)
                pe.wait_ge(ulhs_ready, 2)
                for c in range(2):
                    last = nc.tensor.matmul(ups[:, c * P:(c + 1) * P], ulhs[:, c, :], idf[:, :],
                                            start=True, stop=True)
                last.then_inc(ups_ready, 1)

                def pack(t, b, first):
                    if not first:
                        pe.wait_ge(pk_ready, t - 1)
                    for q in range(Q):
                        pe.wait_ge(conv_done, t * Q + q + 1)
                        for jb in range(q * QB, (q + 1) * QB):
                            last = nc.tensor.matmul(pkps[b][:, jb * WPB:(jb + 1) * WPB],
                                                    adj_f[:, b, jb * P:(jb + 1) * P], packw[:, :],
                                                    start=True, stop=True)
                    last.then_inc(pack_done, 1)

                def keys(t, b):
                    pe.wait_ge(adjT_ready, t + 1)
                    if t is not 0:
                        pe.wait_ge(ksg_ready, t * 4)
                    for jb in range(T):
                        at = jb * KPB % (NK // 2)
                        last = nc.tensor.matmul(kps[jb * KPB // (NK // 2)][:, at:at + KPB],
                                                adjT_h[:, b, jb, :], keyw[:, :],
                                                start=True, stop=True)
                    last.then_inc(keys_ps, 1)

                def transpose_agg(t):
                    pe.wait_ge(agg_ready, t + 1)
                    for c in range(2):
                        last = nc.tensor.transpose(tps[:, c * P:(c + 1) * P],
                                                   agg[:, c * P:(c + 1) * P], idf[:, :])
                    last.then_inc(tr_ready, 1)

                def project(t):
                    pe.wait_ge(aggT_ready, t + 1)
                    for c in range(2):
                        last = nc.tensor.matmul(yps[:, 0:D], aggT[:, c, :], w_sb[:, c, :],
                                                start=(c == 0), stop=(c == 1))
                    last.then_inc(y_ready, 1)

                def aggregate(t, b, v0_wait=False, reuse=True, tail=True, half_way=None):
                    pe.wait_ge(adjT_ready, t + 1)
                    if reuse:
                        pe.wait_ge(agg_ready, t - 1)
                    for jb in range(T):
                        if v0_wait:
                            pe.wait_ge(v0_ready, jb + 1)
                        for s in range(2):
                            last = nc.tensor.matmul(acc[b][:, 0:DV], adjT_h[:, b, jb, :],
                                                    V0[:, jb, s, 0:DV], start=(jb == 0 and s == 0),
                                                    stop=(jb == T - 1 and s == 1))
                        if half_way and jb == T // 2:
                            half_way()
                        if tail and jb == T // 4:
                            transpose_agg(t - 1)
                        if tail and jb == 3 * T // 4:
                            project(t - 1)
                    last.then_inc(acc_ready, 1)

                pack(0, 0, True)
                pe.wait_ge(ubc_ready, 1)
                keys(0, 0)
                pack(1, 1, True)
                aggregate(0, 0, v0_wait=True, reuse=False, tail=False)
                aggregate(1, 1, reuse=False, half_way=lambda: (pack(2, 0, False), keys(1, 1)))
                with pe.Fori(1, NS // 2) as k:
                    for b in range(2):
                        pack(k * 2 + b + 1, (b + 1) % 2, False)
                        keys(k * 2 + b, b)
                        aggregate(k * 2 + b, b)
                with pe.Fori(NS // 2, T // 2 - 1) as k:
                    for b in range(2):
                        pack(k * 2 + b + 1, (b + 1) % 2, False)
                        aggregate(k * 2 + b, b)
                pack(T - 1, 1, False)
                aggregate(T - 2, 0)
                aggregate(T - 1, 1)
                transpose_agg(T - 1)
                project(T - 1)

        G = 4
        NG = T // G
        NGD = SP0 // G
        GC = G * P
        CB = 4
        NC = T // CB
        HS = 4
        GB = 8
        NB = SLOTS // GB
        GT = NS // NGD
        BIG = 2.0 ** 100
        SURE = 12
        STEP = 3
        CT = NC // GT
        assert CT == NB + 1
        assert GT == 4
        LATE = 2
        ctx = ExitStack()
        with ctx:
            def sb(name, shape, dt):
                return ctx.enter_context(nc.sbuf_tensor(name, shape, dt))

            def sem(name):
                return ctx.enter_context(nc.semaphore(name))

            Vp = sb("Vp", [P, T, 2, ROW], f16)
            Vn = sb("Vn", [P, T, 2, ROW], f16)
            adjp = sb("adjp", [P, 2, CB, GC], u16)
            adjp_h = adjp[:, :, :, :].bitcast(f16)
            adjn = sb("adjn", [P, 2, CB, GC], u16)
            adjn_h = adjn[:, :, :, :].bitcast(f16)
            adjn_b = adjn[:, :, :, :].bitcast(bf16)
            pkg = sb("pkg", [P, 2, G, T * WPB], u16)
            h1bc = sb("h1bc", [P, 2, GC], f32)
            hs = sb("hs", [P, HS, ROW], f32)
            x1g = sb("x1g", [P, G, D], f32)
            evp = sb("evp", [P, G, DV], f32)
            evn = hs[:, :, 0:DV]
            gat = sb("gat", [P, NB, GB, ROW], f32)
            sacc = sb("sacc", [P, 2, DV], f32)
            x1s = sb("x1s", [P, 2, D], f32)
            ix = sb("ix", [P, 2, SLOTS], i32)
            e8 = sb("e8", [P, 2, 2, GB], f32)
            m8 = sb("m8", [P, GB], f32)
            w8 = sb("w8", [P, 2, GB], f32)
            hb = sb("hb", [P, 2, T + 1], f32)
            hbt = sb("hbt", [P, 2, 2], f32)
            srd = sb("srd", [P, 1], f32)
            h1T = sb("h1T", [T, P], f32)
            M1 = sb("M1", [P, 4], f32)
            red_in = sb("red_in", [P, NS + 2], f32)
            red = sb("red", [P, NS + 2], f32)
            redi = sb("redi", [P, NS + 2], i32)
            pdum = sb("pdum", [P, 2], f32)
            E = sb("E", [P, 2, T], f32)
            Es = sb("Es", [P, 2, T], f32)
            nh2 = sb("nh2", [P, T], f32)
            sM = sb("sM", [P, 2, T], f32)
            tM = sb("tM", [P, T], f32)
            dM = sb("dM", [P, 2, T], f32)
            ab = sb("ab", [P, 2, T], f32)
            den2 = sb("den2", [P, 2, G], f32)
            den = sb("den", [P, G], f32)
            rd = sb("rd", [P, G], f32)
            fac = sb("fac", [P, 2, G], f32)

            h_in = [sem(f"h_in{i}") for i in range(HS)]
            pkg_in = [sem(f"pkg_in{i}") for i in range(2)]
            h1bc_in = [sem(f"h1bc_in{i}") for i in range(2)]
            x1g_in = sem("x1g_in")
            h1T_ps = sem("h1T_ps")
            h1T_sb = sem("h1T_sb")
            h1_out = sem("h1_out")
            mx_ready = sem("mx_ready")
            M_all = sem("M_all")
            redi_ready = sem("redi_ready")
            gat_zero = sem("gat_zero")
            nh2_ready = sem("nh2_ready")
            negM_ready = sem("negM_ready")
            E_ready = sem("E_ready")
            Es_ready = sem("Es_ready")
            sM_ready = sem("sM_ready")
            s01_ready = sem("s01_ready")
            tM_ready = sem("tM_ready")
            dM_ready = sem("dM_ready")
            ab_ready = sem("ab_ready")
            vhi1_ready = sem("vhi1_ready")
            v_ready = sem("v_ready")
            sign_ready = sem("sign_ready")
            bits_ready = sem("bits_ready")
            pos_ready = sem("pos_ready")
            neg_ready = sem("neg_ready")
            chunk_used = sem("chunk_used")
            evp_ready = sem("evp_ready")
            evn_ready = sem("evn_ready")
            den2_ready = sem("den2_ready")
            den_ready = sem("den_ready")
            rd_ready = sem("rd_ready")
            fac_ready = sem("fac_ready")
            on_ready = sem("on_ready")
            op_ready = sem("op_ready")
            o_ready = sem("o_ready")
            o_out = sem("o_out")
            ix_ready = sem("ix_ready")
            gathered = sem("gathered")
            pdum_done = sem("pdum_done")
            gat_in = [sem(f"gat_in{i}") for i in range(NB)]
            e8_ready = sem("e8_ready")
            m8_ready = sem("m8_ready")
            w8_ready = sem("w8_ready")
            hb_ready = sem("hb_ready")
            sacc_ready = sem("sacc_ready")
            row_added = sem("row_added")
            srd_ready = sem("srd_ready")
            so_ready = sem("so_ready")
            x1s_in = [sem(f"x1s_in{i}") for i in range(2)]
            so_out = [sem(f"so_out{i}") for i in range(2)]

            block = ctx.enter_context(nc.Block())

            @block.sync
            def _(sp):
                def load_words(g, b):
                    sp.dma_start(pkg[:, b, :, :], pk_d[bass.ds(g * G, G), :, :]
                                 .rearrange("g p n -> p g n")).then_inc(pkg_in[b], 16)

                def load_h1(g, b):
                    sp.dma_start(h1bc[:, b, :], h1_d[bass.ds(g * G, G), :]
                                 .rearrange("g p -> (g p)").rearrange("(o n) -> o n", o=1)
                                 .partition_broadcast(P)).then_inc(h1bc_in[b], 16)

                for b in range(HS):
                    sp.dma_start(hs[:, b, :], h_d[b]).then_inc(h_in[b], 16)
                load_words(0, 0)
                sp.wait_ge(h1T_sb, 1)
                sp.dma_start(h1_d, h1T[:, :]).then_inc(h1_out, 16)
                sp.wait_ge(h1_out, 16)
                load_h1(0, 0)
                load_words(1, 1)
                load_h1(1, 1)
                with sp.Fori(1, T // HS) as k:
                    for b in range(HS):
                        sp.wait_ge(v_ready, (k - 1) * (2 * HS) + 2 * b + 2)
                        sp.dma_start(hs[:, b, :], h_d[bass.ds(k * HS + b, 1), :, :]
                                     .rearrange("o p n -> p (o n)")).then_inc(h_in[b], 16)

                def group(g, b, ahead, first):
                    if not first:
                        sp.wait_ge(o_out, g * 16)
                    sp.dma_start(x1g[:, :, :], x1_d[bass.ds(g * G, G), :, :]
                                 .rearrange("g p n -> p g n")).then_inc(x1g_in, 16)
                    if ahead:
                        sp.wait_ge(bits_ready, g * NC + NC)
                        load_words(g + 2, b)
                        sp.wait_ge(sign_ready, g * NC + NC)
                        load_h1(g + 2, b)
                    sp.wait_ge(o_ready, g * G + G)
                    sp.dma_start(out_v[:, bass.ds(g * G, G), :], x1g[:, :, :]).then_inc(o_out, 16)

                group(0, 0, True, True)
                group(1, 1, True, False)
                with sp.Fori(1, NGD // 2 - 1) as k:
                    for b in range(2):
                        group(k * 2 + b, b, True, False)
                group(NGD - 2, 0, False, False)
                group(NGD - 1, 1, False, False)
                sp.wait_ge(o_out, NGD * 16)
                for b in range(2):
                    sp.wait_ge(so_out[b], NS // 2 * 16)
                with sp.If(sp.value_load(redi[0:1, NS + 1:NS + 2]) > 0):
                    load_words(NGD, 0)
                    load_words(NGD + 1, 1)
                    load_h1(NGD, 0)
                    load_h1(NGD + 1, 1)
                    with sp.Fori(NGD // 2, NG // 2 - 1) as k:
                        for b in range(2):
                            group(k * 2 + b, b, True, False)
                    group(NG - 2, 0, False, False)
                    group(NG - 1, 1, False, False)
                    sp.wait_ge(o_out, NG * 16)

            @block.gpsimd
            def _(pool):
                pool.wait_ge(mx_ready, 1)
                nc.gpsimd.partition_all_reduce(red[:, :], red_in[:, :], P, RMAX).then_inc(M_all, 1)
                for i in range(SURE // GB, NB):
                    nc.gpsimd.memset(gat[:, i, max(SURE - i * GB, 0):GB, :], 0.0).then_inc(gat_zero, 1)
                nc.gpsimd.memset(pdum[:, :], 0.0).then_inc(gat_zero, 1)
                pool.wait_ge(redi_ready, 1)
                pool.wait_ge(gat_zero, NB - SURE // GB + 1)
                h_rows = h_d.rearrange("t p n -> (t p) n")
                fetched = [pool.alloc_register(f"fetched{r}") for r in range(NB)]
                for r in range(NB):
                    pool.reg_mov(fetched[r], 0)

                def batch_complete(r):
                    pool.wait_ge(gat_in[r], pool.snap(fetched[r]))
                    pool.sem_inc(gathered, 1)

                def gather_tile(m, b, first):
                    count = pool.value_load(redi[0:1, bass.ds(m, 1)])
                    for i in range(NB):
                        pool.wait_ge(ix_ready, m + 1)
                        if not first:
                            pool.wait_ge(row_added, (m - 1) * SLOTS + (i + 1) * GB)
                        if not first or i:
                            pool.wait_ge(pdum_done, m * NB + i)
                        nc.gpsimd.tensor_tensor(pdum[:, 0:1], pdum[:, 1:2], pdum[:, 1:2], ALU.mult)\
                            .then_inc(pdum_done, 1)

                        def fetch(slots):
                            for s in slots:
                                pool.indirect_dma_start(
                                    gat[:, i, s - i * GB, :], None, h_rows,
                                    bass.IndirectOffsetOnAxis(ap=ix[:, b, s:s + 1], axis=0))\
                                    .then_inc(gat_in[i], 16)
                            pool.reg_add(fetched[i], fetched[i], 16 * len(slots))

                        def fetch_if(s0, s1):
                            with pool.If(count > s0):
                                fetch(range(s0, s1))

                        s = i * GB
                        end = s + GB
                        told = first and i == 0
                        while s < end:
                            if s < SURE:
                                e = min(end, SURE, s + STEP)
                                fetch(range(s, e))
                            else:
                                e = min(end, s + STEP - (s - SURE) % STEP)
                                fetch_if(s, e)
                            s = e
                            if not told:
                                batch_complete((i - 1) % NB)
                                told = True

                gather_tile(0, 0, True)
                gather_tile(1, 1, False)
                with pool.Fori(1, NS // 2) as k:
                    for b in range(2):
                        gather_tile(k * 2 + b, b, False)
                batch_complete(NB - 1)

            @block.scalar
            def _(act):
                for b in range(2):
                    act.dma_start(x1s[:, b, :], x1_d[SP0 + b]).then_inc(x1s_in[b], 16)
                act.wait_ge(negM_ready, 2)
                nc.scalar.activation(E[:, 0, :], h2all[:, :], ACT.Exp, bias=M1[:, 2:3])\
                    .then_inc(E_ready, 1)
                nc.scalar.activation(E[:, 1, :], h2all[:, :], ACT.Exp, scale=SLOPE1, bias=M1[:, 3:4])\
                    .then_inc(E_ready, 1)
                act.wait_ge(dM_ready, 2)
                nc.scalar.activation(ab[:, :, :], dM[:, :, :], ACT.Exp).then_inc(ab_ready, 1)
                act.wait_ge(Es_ready, 1)

                def high_halves(t, j, n_in):
                    act.wait_ge(h_in[j], n_in)
                    for s, V in ((0, Vp), (1, Vn)):
                        nc.scalar.activation(V[:, t, 0, :], hs[:, j, :], ACT.Copy,
                                             scale=Es[:, s, t:t + 1]).then_inc(vhi1_ready, 1)

                def signs(n, b, g2, c, reuse):
                    if reuse:
                        act.wait_ge(chunk_used, n - 1)
                    for jb in range(CB):
                        j = c * CB + jb
                        i = nc.scalar.activation(adjn_b[:, b, jb, :], h1bc[:, g2, :], ACT.Relu,
                                                 scale=-BIG, bias=nh2[:, j:j + 1])
                    i.then_inc(sign_ready, 1)

                def sums(g, first):
                    act.wait_ge(chunk_used, g * NC + NC)
                    if not first:
                        act.wait_ge(op_ready, g * G)
                    for i in range(G):
                        nc.scalar.activation(evn[:, i, :], bank[2 * i + 1][:, 0:DV], ACT.Copy)\
                            .then_inc(evn_ready, 1)

                def scale_sums(g):
                    act.wait_ge(fac_ready, g * 2 + 2)
                    act.wait_ge(evn_ready, g * G + G)
                    for i in range(G):
                        nc.scalar.activation(evn[:, i, 0:D], evn[:, i, 0:D], ACT.Copy,
                                             scale=fac[:, 1, i:i + 1]).then_inc(on_ready, 1)

                def weights(q, i):
                    act.wait_ge(gathered, q + 1)
                    if q is not 0 and q is not 1:
                        act.wait_ge(m8_ready, q - 1)
                    for k, scale in ((0, 1.0), (1, SLOPE1)):
                        nc.scalar.activation(e8[:, i % 2, k, :], gat[:, i % NB, :, DV], ACT.Exp, scale=scale,
                                             bias=hbt[:, i // NB % 2, k:k + 1]).then_inc(e8_ready, 1)

                def start_sums(m, k, none_before):
                    act.wait_ge(w8_ready, m * NB + 1)
                    if not none_before:
                        act.wait_ge(so_ready, m)
                    for s in range(2):
                        nc.scalar.activation(sacc[:, s, :], gat[:, 0, s, 0:DV], ACT.Copy,
                                             scale=w8[:, k % 2, s:s + 1]).then_inc(row_added, 1)

                def tile_out(m, b, fill=True):
                    act.wait_ge(so_ready, m + 1)
                    act.dma_start(out_v[:, bass.ds(m + SP0, 1), :].rearrange("p o n -> p (o n)"),
                                  x1s[:, b, :]).then_inc(so_out[b], 16)
                    if fill:
                        act.wait_ge(so_out[1 - b], (m - 1 - (1 - b)) * 8 + 16)
                        act.dma_start(x1s[:, 1 - b, :], x1_d[bass.ds(m + SP0 + 1, 1), :, :]
                                      .rearrange("o p n -> p (o n)")).then_inc(x1s_in[1 - b], 16)

                def group(g, g2, next_in, first=False):
                    if first:
                        signs(0, 0, 0, 0, False)
                    for c in range(NC):
                        if first:
                            for j in range(CB):
                                high_halves(c * CB + j, j % HS, (c * CB + j) // HS * 16 + 16)
                        if c % CT:
                            k = c // CT * NB + c % CT - 1
                            weights(k if first else g * (GT * NB) + k, k)
                            if k % NB == 0:
                                start_sums(g * GT + c // CT, k, first and k == 0)
                        if c < NC - 1:
                            signs(g * NC + c + 1, (c + 1) % 2, g2, c + 1, not first or c >= 1)
                        if c == CT + 1 and not first:
                            scale_sums(g - 1)
                        if c % CT == 0 and (c or not first):
                            t = c // CT - 1
                            tile_out(g * GT + t, t % 2, not (first and t == 0))
                    if next_in is not None:
                        act.wait_ge(h1bc_in[1 - g2], next_in)
                        signs(g * NC + NC, 0, 1 - g2, 0, True)
                    sums(g, first)

                act.wait_ge(nh2_ready, 1)
                act.wait_ge(h1bc_in[0], 16)
                group(0, 0, 16, first=True)
                group(1, 1, 32)
                with act.Fori(1, NGD // 2 - 1) as k:
                    group(k * 2, 0, k * 16 + 16)
                    group(k * 2 + 1, 1, k * 16 + 32)
                group(NGD - 2, 0, NGD // 2 * 16)
                group(NGD - 1, 1, None)
                tile_out(NS - 1, 1, False)
                scale_sums(NGD - 1)
                with act.If(act.value_load(redi[0:1, NS + 1:NS + 2]) > 0):
                    def dense(g, g2, n_in, tail):
                        act.wait_ge(h1bc_in[g2], n_in)
                        for c in range(NC):
                            signs(g * NC + c, c % 2, g2, c, True)
                            if c == 2 and tail:
                                scale_sums(g - 1)
                        sums(g, False)

                    dense(NGD, 0, NGD * 8 + 16, False)
                    dense(NGD + 1, 1, NGD * 8 + 16, True)
                    with act.Fori(NGD // 2 + 1, NG // 2) as k:
                        for b in range(2):
                            dense(k * 2 + b, b, k * 16 + 16, True)
                    scale_sums(NG - 1)

            @block.vector
            def _(dve):
                nc.vector.tensor_copy(red_in[:, 0:NS], cnt[:, :])
                nc.vector.reduce_max(red_in[:, NS:NS + 1], h2all[:, :], AX.X)
                nc.vector.reduce_max(red_in[:, NS + 1:NS + 2], full[:, :], AX.X).then_inc(mx_ready, 1)
                dve.wait_ge(h1T_ps, 1)
                nc.vector.tensor_copy(h1T[:, :], bank[7][0:T, 0:P]).then_inc(h1T_sb, 1)
                nc.vector.tensor_scalar(nh2[:, :], h2all[:, :], -BIG, None, ALU.mult)\
                    .then_inc(nh2_ready, 1)
                def indices(m, b):
                    nc.vector.tensor_copy(hbt[:, b, :], hb[:, :, bass.ds(m + SP0, 1)]
                                          .rearrange("p k o -> p (k o)"))
                    nc.vector.tensor_scalar(ix[:, b, :], cand[:, bass.ds(m, 1), :]
                                            .rearrange("p o s -> p (o s)"), -1.0, 0.0, ALU.add,
                                            ALU.max).then_inc(ix_ready, 1)

                nc.vector.memset(cand[:, NS:NS + 1, :], 0.0)
                nc.vector.memset(hb[:, :, T:T + 1], 0.0)
                dve.wait_ge(M_all, 1)
                nc.vector.tensor_copy(redi[:, 0:NS], red[:, 0:NS])
                nc.vector.tensor_scalar(redi[:, NS + 1:NS + 2], red[:, NS + 1:NS + 2], 0.0, None,
                                        ALU.is_gt).then_inc(redi_ready, 1)
                Mh = red[:, NS:NS + 1]
                nc.vector.tensor_scalar(M1[:, 2:3], Mh, -1.0, None, ALU.mult).then_inc(negM_ready, 1)
                nc.vector.tensor_scalar(M1[:, 3:4], Mh, -SLOPE1, None, ALU.mult)\
                    .then_inc(negM_ready, 1)
                dve.wait_ge(negM_ready, 2)
                nc.vector.tensor_scalar(sM[:, 0, :], h1all[:, :], Mh, None, ALU.add)\
                    .then_inc(sM_ready, 1)
                dve.wait_ge(sM_ready, 1)
                nc.vector.tensor_scalar(sM[:, 1, :], sM[:, 0, :], SLOPE1, None, ALU.mult)\
                    .then_inc(s01_ready, 1)
                dve.wait_ge(s01_ready, 1)
                nc.vector.tensor_tensor(tM[:, :], sM[:, 0, :], sM[:, 1, :], ALU.max).then_inc(tM_ready, 1)
                dve.wait_ge(tM_ready, 1)
                for s in range(2):
                    nc.vector.tensor_tensor(dM[:, s, :], sM[:, s, :], tM[:, :], ALU.subtract)\
                        .then_inc(dM_ready, 1)
                dve.wait_ge(dM_ready, 2)
                for s in range(2):
                    nc.vector.tensor_scalar(hb[:, s, 0:T], dM[:, s, :], M1[:, 2 + s:3 + s], None, ALU.add)\
                        .then_inc(hb_ready, 1)
                dve.wait_ge(hb_ready, 2)
                indices(0, 0)
                dve.wait_ge(E_ready, 2)
                nc.vector.tensor_scalar(Es[:, :, :], E[:, :, :], VS, None, ALU.mult).then_inc(Es_ready, 1)
                dve.wait_ge(Es_ready, 1)

                def low_halves(t, j):
                    for s, V in ((0, Vp), (1, Vn)):
                        dve.wait_ge(vhi1_ready, 2 * t + s + 1)
                        nc.vector.scalar_tensor_tensor(V[:, t, 1, :], hs[:, j, :],
                                                       Es[:, s, t:t + 1], V[:, t, 0, :],
                                                       ALU.mult, ALU.subtract).then_inc(v_ready, 1)

                def split_chunk(n, b, g2, c, reuse, between=((), ())):
                    if reuse:
                        dve.wait_ge(chunk_used, n - 1)
                    words = pkg[:, g2, :, :].rearrange("p g (t w) -> p t g w", w=WPB)
                    for k in range(BITS):
                        dst = adjp[:, b, :, :].rearrange("p t (g i) -> p t g i", g=G)\
                            [:, :, :, k * WPB:(k + 1) * WPB]
                        src = words[:, c * CB:(c + 1) * CB, :, :]
                        if k <= 14:
                            i = nc.vector.tensor_scalar(dst, src, 1 << k, 14 - k, ALU.bitwise_and,
                                                        ALU.logical_shift_left)
                        else:
                            i = nc.vector.tensor_scalar(dst, src, 1 << k, k - 14, ALU.bitwise_and,
                                                        ALU.logical_shift_right)
                    i.then_inc(bits_ready, 1)
                    both = adjp[:, b, :, :].rearrange("p t i -> p (t i)")
                    part = adjn[:, b, :, :].rearrange("p t i -> p (t i)")
                    for step in between[0]:
                        step()
                    dve.wait_ge(bits_ready, n + 1)
                    dve.wait_ge(sign_ready, n + 1)
                    nc.vector.tensor_tensor(part, both, part, ALU.bitwise_and).then_inc(neg_ready, 1)
                    for step in between[1]:
                        step()
                    dve.wait_ge(neg_ready, n + 1)
                    nc.vector.tensor_tensor(both, both, part, ALU.bitwise_xor).then_inc(pos_ready, 1)

                def take_sums(g):
                    dve.wait_ge(chunk_used, g * NC + NC)
                    for i in range(G):
                        nc.vector.tensor_copy(evp[:, i, :], bank[2 * i][:, 0:DV]).then_inc(evp_ready, 1)

                def factors(g):
                    dve.wait_ge(evp_ready, g * G + G)
                    dve.wait_ge(evn_ready, g * G + G)
                    for s, ev in ((0, evp), (1, evn)):
                        nc.vector.tensor_tensor(den2[:, s, :], ab[:, s, bass.ds(g * G, G)],
                                                ev[:, :, D], ALU.mult).then_inc(den2_ready, 1)
                    dve.wait_ge(den2_ready, g * 2 + 2)
                    nc.vector.tensor_tensor(den[:, :], den2[:, 0, :], den2[:, 1, :], ALU.add)\
                        .then_inc(den_ready, 1)
                    dve.wait_ge(den_ready, g + 1)
                    nc.vector.reciprocal(rd[:, :], den[:, :]).then_inc(rd_ready, 1)
                    dve.wait_ge(rd_ready, g + 1)
                    for s in range(2):
                        nc.vector.tensor_tensor(fac[:, s, :], ab[:, s, bass.ds(g * G, G)], rd[:, :],
                                                ALU.mult).then_inc(fac_ready, 1)

                def add_parts(g):
                    dve.wait_ge(fac_ready, g * 2 + 2)
                    for i in range(G):
                        dve.wait_ge(on_ready, g * G + i + 1)
                        nc.vector.scalar_tensor_tensor(evp[:, i, 0:D], evp[:, i, 0:D],
                                                       fac[:, 0, i:i + 1], evn[:, i, 0:D],
                                                       ALU.mult, ALU.add).then_inc(op_ready, 1)

                def add_x1(g):
                    dve.wait_ge(x1g_in, g * 16 + 16)
                    for i in range(G):
                        dve.wait_ge(op_ready, g * G + i + 1)
                        nc.vector.tensor_tensor(x1g[:, i, :], x1g[:, i, :], evp[:, i, 0:D], ALU.add)\
                            .then_inc(o_ready, 1)

                def larger(q, k):
                    dve.wait_ge(e8_ready, 2 * q + 2)
                    nc.vector.tensor_tensor(m8[:, :], e8[:, k % 2, 0, :], e8[:, k % 2, 1, :],
                                            ALU.max).then_inc(m8_ready, 1)

                def mask_weights(q, k, m):
                    i = k % NB
                    dve.wait_ge(m8_ready, q + 1)
                    nc.vector.scalar_tensor_tensor(
                        w8[:, k % 2, :], cand[:, bass.ds(m, 1), i * GB:(i + 1) * GB]
                        .rearrange("p o s -> p (o s)"), 0.0, m8[:, :], ALU.is_gt, ALU.mult)\
                        .then_inc(w8_ready, 1)

                def add_row(q, k, s):
                    i = k % NB
                    row, w, acc = gat[:, i, s, 0:DV], w8[:, k % 2, s:s + 1], sacc[:, s % 2, :]
                    dve.wait_ge(row_added, q * GB + (2 if i == 0 and s == 2 else s - 1))
                    nc.vector.scalar_tensor_tensor(acc, row, w, acc, ALU.mult, ALU.add)\
                        .then_inc(row_added, 1)

                def tile_finish(m, b, n_in):
                    dve.wait_ge(row_added, m * SLOTS + SLOTS)
                    nc.vector.tensor_tensor(sacc[:, 0, :], sacc[:, 0, :], sacc[:, 1, :], ALU.add)\
                        .then_inc(sacc_ready, 1)
                    dve.wait_ge(sacc_ready, m + 1)
                    nc.vector.reciprocal(srd[:, :], sacc[:, 0, D:DV]).then_inc(srd_ready, 1)
                    dve.wait_ge(srd_ready, m + 1)
                    dve.wait_ge(x1s_in[b], n_in)
                    nc.vector.scalar_tensor_tensor(x1s[:, b, :], sacc[:, 0, 0:D], srd[:, :],
                                                   x1s[:, b, :], ALU.mult, ALU.add)\
                        .then_inc(so_ready, 1)

                def group(g, g2, n_in, first=False):
                    dve.wait_ge(pkg_in[g2], n_in)
                    for c in range(NC):
                        k = (c - 1) // CT * NB + (c - 1) % CT
                        q = g * (GT * NB) + k
                        m = g * GT + c // CT
                        late = ([], [])
                        if c % CT:
                            late[0].append(lambda: larger(q, k))
                            late[1].append(lambda: mask_weights(q, k, m))
                        if c % CT != 1 and (c or not first):
                            for a in range(2):
                                late[a].append(lambda s=GB - LATE + a: add_row(q - 1, k - 1, s))
                        if c % CT == 1:
                            late[0].append(lambda: indices(m + 1, (c // CT + 1) % 2))
                        split_chunk(g * NC + c, c % 2, g2, c, not first or c >= 2, late)
                        if first:
                            for j in range(CB):
                                low_halves(c * CB + j, j % HS)
                        if not first and c % CT == 0:
                            (take_sums, factors, add_parts, add_x1)[c // CT](g - 1)
                        if c % CT:
                            dve.wait_ge(w8_ready, q + 1)
                            for s in range(0 if k % NB else 2, GB - LATE):
                                add_row(q, k, s)
                        elif c or not first:
                            m = g * GT + c // CT - 1
                            b = (c // CT - 1) % 2
                            tile_finish(m, b, (m - b) * 8 + 16)

                dve.wait_ge(ab_ready, 1)
                group(0, 0, 16, first=True)
                group(1, 1, 16)
                with dve.Fori(1, NGD // 2) as k:
                    for g2 in range(2):
                        group(k * 2 + g2, g2, k * 16 + 16)
                for s in range(GB - LATE, GB):
                    add_row(NS * NB - 1, GT * NB - 1, s)
                tile_finish(NS - 1, 1, NS // 2 * 16)
                for part in (take_sums, factors, add_parts, add_x1):
                    part(NGD - 1)
                with dve.If(dve.value_load(redi[0:1, NS + 1:NS + 2]) > 0):
                    def dense(g, g2, n_in, tail):
                        dve.wait_ge(pkg_in[g2], n_in)
                        for c in range(NC):
                            split_chunk(g * NC + c, c % 2, g2, c, True)
                            if c < 4 and tail:
                                (take_sums, factors, add_parts, add_x1)[c](g - 1)

                    dense(NGD, 0, NGD * 8 + 16, False)
                    dense(NGD + 1, 1, NGD * 8 + 16, True)
                    with dve.Fori(NGD // 2 + 1, NG // 2) as k:
                        for g2 in range(2):
                            dense(k * 2 + g2, g2, k * 16 + 16, True)
                    for part in (take_sums, factors, add_parts, add_x1):
                        part(NG - 1)

            @block.tensor
            def _(pe):
                nc.tensor.transpose(bank[7][0:T, 0:P], h1all[:, :], idf[:, :]).then_inc(h1T_ps, 1)

                def group(g, first):
                    for c in range(NC):
                        n = g * NC + c
                        b = c % 2
                        pe.wait_ge(pos_ready, n + 1)
                        for jb in range(CB):
                            j = c * CB + jb
                            if first:
                                pe.wait_ge(v_ready, 2 * j + 2)
                            for i in range(G):
                                for part, (m, V) in enumerate(((adjp_h, Vp), (adjn_h, Vn))):
                                    if j == 0:
                                        if first and i == 0 and part == 0:
                                            pe.wait_ge(h1T_sb, 1)
                                        if not first:
                                            pe.wait_ge(evn_ready if part else evp_ready,
                                                       g * G - G + i + 1)
                                    for s in range(2):
                                        last = nc.tensor.matmul(
                                            bank[2 * i + part][:, 0:DV],
                                            m[:, b, jb, i * P:(i + 1) * P], V[:, j, s, 0:DV],
                                            start=(j == 0 and s == 0), stop=(j == T - 1 and s == 1))
                        last.then_inc(chunk_used, 1)

                group(0, True)
                with pe.Fori(1, NGD) as g:
                    group(g, False)
                pe.wait_ge(redi_ready, 1)
                with pe.If(pe.value_load(redi[0:1, NS + 1:NS + 2]) > 0):
                    with pe.Fori(NGD, NG) as g:
                        group(g, False)


_INS = ['x', 'adj', 'L0_gnn_W', 'L0_gnn_a', 'L1_gnn_a']


def kernel(**inputs):
    import numpy as np
    import concourse.bacc as bacc
    from concourse import mybir as _mybir
    from concourse.bass_utils import run_bass_kernel_spmd as run

    nc = bacc.Bacc("TRN2", target_bir_lowering=False, num_devices=1)
    arrays, args = {}, []

    def add(name, a):
        arrays[name] = a
        args.append(nc.dram_tensor(name, a.shape, _mybir.dt.from_np(a.dtype), kind="ExternalInput").ap())

    for name in _INS:
        add(f"in_{name}", np.ascontiguousarray(inputs[name]))
    rows = np.arange(128)
    pack_w = np.zeros((128, 8), np.float16)
    pack_w[rows, rows % 8] = 2.0 ** (rows // 8)
    add("pack_w", pack_w)
    key_w = np.zeros((128, 16), np.float16)
    key_w[rows, rows // 8] = 2.0 ** (rows % 8 - 1)
    add("key_w", key_w)
    add("key_pos", np.arange(inputs["x"].shape[0] // 8).astype(np.float16))
    add("ident", np.eye(128, dtype=np.float32))
    out = nc.dram_tensor("out", inputs["x"].shape, _mybir.dt.float32, kind="ExternalOutput").ap()
    two_layer_graph_attention(nc, *args, out)
    r = run(nc, [arrays], core_ids=[0])
    return r.results[0]["out"]
```
